# Optimizing a Trainium2 kernel written in Bass

```python
import numpy as np
import jax
import jax.numpy as jnp

def _softmax(x, axis=-1):
    return jax.nn.softmax(x, axis=axis)

def _gelu(x):
    return jax.nn.gelu(x, approximate=True)

def _silu(x):
    return jax.nn.silu(x)

def _sigmoid(x):
    return jax.nn.sigmoid(x)

def _layernorm(x, axis=-1, eps=1e-05):
    m = jnp.mean(x, axis=axis, keepdims=True)
    v = jnp.var(x, axis=axis, keepdims=True)
    return (x - m) / jnp.sqrt(v + eps)

def _scatter_add(tgt, idx, src, axis=0):
    return tgt.at[idx].add(src)

def _segment_sum(src, seg, n):
    return jax.ops.segment_sum(src, seg, n)
kernel_name = 'mk_vit_tower_d1_tok_img768_r4_0283d1'

def setup_inputs(seed: int=0):
    np.random.seed(seed)
    _w = jnp.asarray

    def _rec_inputs():
        import jax
        import jax.numpy as jnp
        _rk = jax.random.key(seed)
        x = -0.00016672 + 0.999947 * jax.random.normal(jax.random.fold_in(_rk, 1), (64, 3, 224, 224), jnp.float32)
        return x
    x = _rec_inputs()

    def _L0_tok_setup():
        import jax, jax.numpy as jnp
        import numpy as np
        PATCH = 16
        SHIFT = PATCH // 2
        EPS = 1e-05
        key = jax.random.key(seed)
        k1, k2 = jax.random.split(key)
        B, C, H, Wd = (64, 3, 96, 96)
        patch_dim = C * PATCH * PATCH
        dim = 192
        x = jax.random.normal(k1, (B, C, H, Wd), dtype=jnp.float32)
        gamma = jnp.ones((patch_dim,), dtype=jnp.float32)
        beta = jnp.zeros((patch_dim,), dtype=jnp.float32)
        W = jax.random.normal(k2, (dim, patch_dim), dtype=jnp.float32) * patch_dim ** (-0.5)
        b = jnp.zeros((dim,), dtype=jnp.float32)
        return {'x': x, 'gamma': gamma, 'beta': beta, 'W': W, 'b': b}
    _L0_tok_all = _L0_tok_setup()
    _L0_tok_in = {k: v for k, v in _L0_tok_all.items() if k in ('gamma', 'beta', 'W', 'b')}
    del _L0_tok_all

    def _L0_attn_setup():
        import jax, jax.numpy as jnp
        import numpy as np
        B, N, C = (8, 256, 192)
        H = 12
        D = C // H
        SCALE = D ** (-0.5)
        EPS = 1e-05

        def _layer_norm(x):
            mean = x.mean(-1, keepdims=True)
            var = ((x - mean) ** 2).mean(-1, keepdims=True)
            return (x - mean) / jnp.sqrt(var + EPS)
        key = jax.random.key(seed)
        k1, k2, k3 = jax.random.split(key, 3)
        x = jax.random.normal(k1, (B, N, C), dtype=jnp.float32)
        qkv_weight = jax.random.normal(k2, (3 * C, C), dtype=jnp.float32) * C ** (-0.5)
        proj_weight = jax.random.normal(k3, (C, C), dtype=jnp.float32) * C ** (-0.5)
        return {'x': x, 'qkv_weight': qkv_weight, 'proj_weight': proj_weight}
    _L0_attn_all = _L0_attn_setup()
    _L0_attn_in = {k: v for k, v in _L0_attn_all.items() if k in ('qkv_weight', 'proj_weight')}
    del _L0_attn_all

    def _L0_ffn_setup():
        import jax, jax.numpy as jnp
        import numpy as np
        B, T, H, F, E = (128, 32, 192, 768, 3)
        key = jax.random.key(seed)
        ks = jax.random.split(key, 4)
        s = 0.02
        return {'x': jax.random.normal(ks[0], (B, T, H), jnp.float32), 'Wg': jax.random.normal(ks[1], (E, H), jnp.float32) * s, 'W1': jax.random.normal(ks[2], (E, H, F), jnp.float32) * s, 'b1': jnp.zeros((E, F), jnp.float32), 'W2': jax.random.normal(ks[3], (E, F, H), jnp.float32) * s, 'b2': jnp.zeros((E, H), jnp.float32)}
    _L0_ffn_all = _L0_ffn_setup()
    _L0_ffn_in = {k: v for k, v in _L0_ffn_all.items() if k in ('Wg', 'W1', 'b1', 'W2', 'b2')}
    del _L0_ffn_all
    return {'x': x, 'L0_tok_gamma': _L0_tok_in['gamma'], 'L0_tok_beta': _L0_tok_in['beta'], 'L0_tok_W': _L0_tok_in['W'], 'L0_tok_b': _L0_tok_in['b'], 'L0_attn_qkv_weight': _L0_attn_in['qkv_weight'], 'L0_attn_proj_weight': _L0_attn_in['proj_weight'], 'L0_ffn_Wg': _L0_ffn_in['Wg'], 'L0_ffn_W1': _L0_ffn_in['W1'], 'L0_ffn_b1': _L0_ffn_in['b1'], 'L0_ffn_W2': _L0_ffn_in['W2'], 'L0_ffn_b2': _L0_ffn_in['b2']}

def reference(x, L0_tok_gamma, L0_tok_beta, L0_tok_W, L0_tok_b, L0_attn_qkv_weight, L0_attn_proj_weight, L0_ffn_Wg, L0_ffn_W1, L0_ffn_b1, L0_ffn_W2, L0_ffn_b2):
    import jax
    import jax.numpy as jnp

    def _L0_tok_ref(x, gamma, beta, W, b):
        import jax, jax.numpy as jnp
        import numpy as np
        PATCH = 16
        SHIFT = PATCH // 2
        EPS = 1e-05
        B, C, H, Wd = x.shape
        s2 = 2 * SHIFT
        xp = jnp.pad(x, ((0, 0), (0, 0), (SHIFT, SHIFT), (SHIFT, SHIFT)))
        x_cat = x + xp[:, :, :-s2, :-s2] + xp[:, :, :-s2, s2:] + xp[:, :, s2:, s2:] + xp[:, :, s2:, :-s2]
        h, w = (H // PATCH, Wd // PATCH)
        t = x_cat.reshape(B, C, h, PATCH, w, PATCH)
        t = t.transpose(0, 2, 4, 3, 5, 1).reshape(B, h * w, PATCH * PATCH * C)
        mu = jnp.mean(t, axis=-1, keepdims=True)
        var = jnp.mean(jnp.square(t - mu), axis=-1, keepdims=True)
        t = (t - mu) * jax.lax.rsqrt(var + EPS) * gamma + beta
        out = jnp.einsum('bnp,dp->bnd', t, W) + b
        return out

    def _L0_attn_ref(x, qkv_weight, proj_weight):
        import jax, jax.numpy as jnp
        import numpy as np
        B, N, C = (8, 256, 192)
        H = 12
        D = C // H
        SCALE = D ** (-0.5)
        EPS = 1e-05

        def _layer_norm(x):
            mean = x.mean(-1, keepdims=True)
            var = ((x - mean) ** 2).mean(-1, keepdims=True)
            return (x - mean) / jnp.sqrt(var + EPS)
        Bx, Nx, Cx = x.shape
        qkv = x @ qkv_weight.T
        qkv = qkv.reshape(Bx, Nx, 3, H, D).transpose(2, 0, 3, 1, 4)
        q, k, v = (qkv[0], qkv[1], qkv[2])
        q = _layer_norm(q) * SCALE
        k = _layer_norm(k)
        attn = jnp.einsum('bhnd,bhmd->bhnm', q, k)
        attn = jax.nn.softmax(attn, axis=-1)
        out = jnp.einsum('bhnm,bhmd->bhnd', attn, v)
        out = out.transpose(0, 2, 1, 3).reshape(Bx, Nx, Cx)
        return out @ proj_weight.T

    def _L0_ffn_ref(x, Wg, W1, b1, W2, b2):
        import jax, jax.numpy as jnp
        import numpy as np
        B, T, H, F, E = (128, 32, 192, 768, 3)
        scores = jax.nn.softmax(jnp.mean(x, axis=1) @ Wg.T, axis=-1)
        _, idx = jax.lax.top_k(scores, 1)
        sel = idx[:, 0]
        h = jax.nn.gelu(jnp.einsum('bth,ehf->betf', x, W1) + b1[None, :, None, :], approximate=False)
        y = jnp.einsum('betf,efh->beth', h, W2) + b2[None, :, None, :]
        w = scores * jax.nn.one_hot(sel, E, dtype=scores.dtype)
        out = jnp.einsum('beth,be->bth', y, w)
        return out
    h = _L0_tok_ref(x, L0_tok_gamma, L0_tok_beta, L0_tok_W, L0_tok_b)
    h = h + _L0_attn_ref(_layernorm(h, axis=-1), L0_attn_qkv_weight, L0_attn_proj_weight)
    h = h + _L0_ffn_ref(_layernorm(h, axis=-1), L0_ffn_Wg, L0_ffn_W1, L0_ffn_b1, L0_ffn_W2, L0_ffn_b2)
    return h

_drawn_inputs = setup_inputs


def setup_inputs(seed=0):
    import zlib

    import numpy as np

    out = dict(_drawn_inputs(seed))
    spreads = {'L0_tok_gamma': (1.0, 0.2),
     'L0_tok_beta': (0.0, 0.1),
     'L0_tok_b': (0.0, 0.1),
     'L0_ffn_b1': (0.0, 0.78),
     'L0_ffn_b2': (0.0, 0.1)}
    factors = {}
    for name, (base, spread) in spreads.items():
        noise = np.random.default_rng([zlib.crc32(name.encode()), seed]).standard_normal(out[name].shape)
        drawn = base * np.exp(spread * noise) if base else spread * noise
        out[name] = jnp.asarray(drawn.astype(out[name].dtype))
    for name, factor in factors.items():
        out[name] = (out[name] * factor).astype(out[name].dtype)
    return out
```

```python
from contextlib import ExitStack

import concourse.bass as bass
from concourse import mybir

F32 = mybir.dt.float32
F16 = mybir.dt.float16
I32 = mybir.dt.int32
ALU = mybir.AluOpType
ACT = mybir.ActivationFunctionType
AX_X = mybir.AxisListType.X

EPS = 1e-5
PATCH = 16
HALF = PATCH // 2
CH = 3
D = 192
HEADS = 12
HD = D // HEADS
HW = 32
KC = 96
NKC = D // KC
E = 3
FF = 768
FC = FF // 128

S_ACT = 32.0
S_W = 256.0
S_QK = 64.0
S_HID = 16.0

EPS_QK = HD * EPS * (S_ACT * S_W) ** 2
NEWTON = 3


class Image:

    def __init__(self, engine, index, parity):
        self.engine, self.index, self.parity, self.kept = engine, index, parity, {}

    def upto(self, d):
        if isinstance(self.index, int):
            return self.index + d + 1
        if d not in self.kept:
            self.kept[d] = self.engine.snap(self.index + (d + 1))
        return self.kept[d]

    def slot(self, d):
        return (self.parity + d) % 2


def wait(engine, sem, count):
    if not isinstance(count, int) or count > 0:
        engine.wait_ge(sem, count)


def build_vit(nc, own, opposite, tokW, tokGamma, tokBeta, tokB, qkvW, projW, gateW, W1, b1, W2, b2, out):
    B = own.shape[0]
    G = own.shape[3]
    CB = own.shape[2]
    SIDE = 14
    T = G // 2
    PD = CH * PATCH * PATCH
    OPP = SIDE + 1

    h1_dram = nc.dram_tensor("h1_scratch", [B, T, 2 * D], F32).ap()
    y2_dram = nc.dram_tensor("y2_scratch", [B, KC, 2 * NKC * G], F16).ap()

    with ExitStack() as ctx:
        def sem(name):
            return ctx.enter_context(nc.semaphore(name))

        WORDS = 54000
        arena = ctx.enter_context(nc.sbuf_tensor("arena", [128, WORDS], F32))
        used = [0]
        peak = [0]

        def take(parts, *dims, dt=F32):
            n = 1
            for x in dims:
                n *= x
            words = n if dt in (F32, I32) else (n + 1) // 2
            words = (words + 7) // 8 * 8
            at = used[0]
            used[0] += words
            peak[0] = max(peak[0], used[0])
            assert used[0] <= WORDS, used[0]
            v = arena[0:parts, at:at + (n if dt in (F32, I32) else n // 2)]
            if dt != F32:
                v = v.bitcast(dt)
            if len(dims) > 1:
                names = [f"d{k}" for k in range(len(dims))]
                v = v.rearrange("p (" + " ".join(names) + ") -> p " + " ".join(names), **dict(zip(names, dims)))
            return v

        ident = take(128, 128)
        ident16 = take(128, 128, dt=F16)
        ones = take(128, 128)
        eps_ln = take(T, 2)
        minus_half = take(T, 2)
        gate_w = take(KC, NKC, E)
        gate_sum = take(KC, B, NKC)
        after_shared = used[0]

        tok_w = take(128, CB, D + 1)
        tok_bias = take(T, D)
        qkv_w = take(KC, 2, NKC, 3 * D, dt=F16)
        proj_w = take(KC, 2, NKC, D, dt=F16)
        own_x = [take(128, CB * G) for _ in range(2)]
        opp_x = [take(128, CB, OPP, OPP) for _ in range(2)]
        row_sum = take(128, CB, SIDE, OPP)
        xcat = [take(128, CB, G) for _ in range(2)]
        xsq = take(128, CB, G)
        xsq_sum = take(128, G)
        tok_mean = take(T, 2)
        tok_mean2 = take(T, 2)
        tok_var = take(T, 2)
        tok_rstd = take(T, 2)
        tok_sh, sh1, sh2 = take(T, 2), take(T, 2), take(T, 2)
        qk_var = take(T, 4 * HEADS)
        qk_t = take(T, 4 * HEADS)
        h0 = [take(T, 2, D) for _ in range(2)]
        h0_ring = take(T, 4 * 2 * D)
        y = take(T, 2, D)
        yT = take(KC, 2, NKC * G, dt=F16)
        bn1 = take(T, 2, 6)
        mv1 = take(T, 2, 2)
        rstd1 = take(T, 2)
        qk_sq = take(T, 2, 2 * D)
        qk_ss = take(T, 4 * HEADS)
        qk_rs = take(T, 4 * HEADS)
        qk_n = take(T, 2, 2 * HEADS, HD)
        q_st = take(T, 2 * HEADS, 4 * HD, dt=F16)
        k_st = take(T, 2 * HEADS, 4 * HD, dt=F16)
        q_even = [take(128, HEADS // 2, G, dt=F16) for _ in range(2)]
        q_odd = [take(128, HEADS // 2, G, dt=F16) for _ in range(2)]
        kT = [take(128, HEADS // 2, G, dt=F16) for _ in range(2)]
        val = [take(T, 2, HEADS, HW) for _ in range(2)]
        prob = [take(T, 2 * G) for _ in range(HEADS)]
        oT = take(128, 3, G)
        rden = take(T, 2, HEADS)
        attn = take(T, 2, D)
        aT = take(KC, 2, NKC * G, dt=F16)
        h1 = [take(T, 2, D) for _ in range(2)]
        bn2 = take(T, 2, 6)
        mv2 = take(T, 2, 2)
        rstd2 = take(T, 2)
        y2 = take(T, 2, D)
        y2T = [take(KC, 2, NKC * G, dt=F16) for _ in range(2)]
        keep = used[0]
        used[0] = keep
        tok_raw = take(128, CB, D)
        tok_gam = take(128, CB)
        tok_bet = take(128, CB)
        beta_cols = take(128, CB, T)
        tok_b = take(T, D)
        qkv_raw = take(KC, NKC, 3 * D)
        qkv_gs = take(KC, NKC, 2 * HEADS)
        proj_raw = take(KC, NKC, D)

        used[0] = after_shared
        w1_raw = take(KC + 1, E, NKC, FF)
        w2_raw = take(128, E, FC, D)
        b2_all = take(T, E * D)
        w1_all = take(KC + 1, E * 2 * NKC * FF, dt=F16)
        w2_all = take(128, E * 2 * FC * D, dt=F16)
        w1_sel = [take(KC + 1, 2, NKC, FF, dt=F16) for _ in range(2)]
        w2_sel = [take(128, 2, FC, D, dt=F16) for _ in range(2)]
        x2 = [take(KC + 1, 2, NKC, G, dt=F16) for _ in range(2)]
        h1_in = [take(T, 2, D) for _ in range(2)]
        hid = [take(128, 2 * G) for _ in range(3)]
        hidT = [take(128, 2, 2 * G, dt=F16) for _ in range(3)]
        y_out = [take(T, 2, D) for _ in range(2)]
        y_fin = [take(T, 2, D) for _ in range(2)]
        g_logit = take(B, E)
        g_max = take(B, 1)
        g_sub = take(B, E)
        g_exp = take(B, E)
        g_sum = take(B, 1)
        g_pair = take(B, 2)
        g_is = take(B, E)
        g_not = take(B, 2)
        g_wide = take(B, 2, T)
        gate = take(T, B)
        expert_f = take(1, B)
        expert = take(1, B, dt=I32)

        bank = [ctx.enter_context(nc.psum_tensor(f"bank{n}", [128, 512], F32)) for n in range(8)]
        S = bank[0:3]
        O = bank[3:5]
        X, Y, Z = bank[5:8]
        X16, Z16 = X[:, :].bitcast(F16), Z[:, :].bitcast(F16)

        def o_bank(image_slot, g):
            return O[(image_slot + g) % 2]

        weights_in = sem("weights_in")
        const_ready = sem("const_ready")
        setup_dve = sem("setup_dve")
        setup_mm = sem("setup_mm")
        weights_ready = sem("weights_ready")
        x_in = [sem(f"x_in{n}") for n in range(2)]
        rows_added = sem("rows_added")
        cols_added = sem("cols_added")
        xcat_ready = sem("xcat_ready")
        xsq_ready = sem("xsq_ready")
        xsq_fold = [sem(f"xsq_fold{n}") for n in range(2)]
        xsq_summed = sem("xsq_summed")
        tok_ready = sem("tok_ready")
        tok_stat = [sem(f"tok_stat{n}") for n in range(4)]
        h0_ready = sem("h0_ready")
        h0_kept = sem("h0_kept")
        ln1_stat = [sem(f"ln1_stat{n}") for n in range(3)]
        y_ready = sem("y_ready")
        yT_ready = sem("yT_ready")
        yT_high = sem("yT_high")
        yT_split = sem("yT_split")
        qkv_ready = [sem(f"qkv_ready{j}") for j in range(2)]
        qk_squared = [sem(f"qk_squared{j}") for j in range(2)]
        qk_summed = sem("qk_summed")
        qk_step = [sem(f"qk_step{n}") for n in range(3 * NEWTON + 2)]
        tok_shifted, ln1_shifted, ln2_shifted = (sem(f"{n}_shifted") for n in ("tok", "ln1", "ln2"))
        qk_normed = sem("qk_normed")
        qk_high = sem("qk_high")
        qk_split = sem("qk_split")
        v_ready = sem("v_ready")
        stack_T = [sem(f"stack_T{r}") for r in range(2)]
        q_ready = [sem(f"q_ready{r}") for r in range(2)]
        k_ready = [sem(f"k_ready{r}") for r in range(2)]
        scores_ready = [sem(f"scores_ready{h}") for h in range(HEADS)]
        prob_ready = [sem(f"prob_ready{h}") for h in range(HEADS)]
        o_ready = [sem(f"o_ready{g}") for g in range(3)]
        o_out = [sem(f"o_out{g}") for g in range(3)]
        o_tokens = sem("o_tokens")
        den_inv = sem("den_inv")
        attn_ready = sem("attn_ready")
        aT_ready = sem("aT_ready")
        aT_high = sem("aT_high")
        aT_split = sem("aT_split")
        proj_ready = sem("proj_ready")
        h1_ready = sem("h1_ready")
        ln2_stat = [sem(f"ln2_stat{n}") for n in range(3)]
        y2_ready = sem("y2_ready")
        y2T_ready = sem("y2T_ready")
        y2T_high = sem("y2T_high")
        y2T_split = sem("y2T_split")
        gate_summed = sem("gate_summed")
        h1_saved = [sem(f"h1_saved{n}") for n in range(2)]
        y2_saved = [sem(f"y2_saved{n}") for n in range(2)]

        experts_in = sem("experts_in")
        rows_set = sem("rows_set")
        experts_split = sem("experts_split")
        logits_ready = sem("logits_ready")
        gate_step = sem("gate_step")
        gate_exp = sem("gate_exp")
        gate_wide = sem("gate_wide")
        gate_ready = sem("gate_ready")
        expert_known = sem("expert_known")
        x2_in = [sem(f"x2_in{n}") for n in range(2)]
        h1_back = [sem(f"h1_back{n}") for n in range(2)]
        w1_chosen = sem("w1_chosen")
        w2_chosen = sem("w2_chosen")
        hid_ready = [sem(f"hid_ready{m}") for m in range(3)]
        hid_act = [sem(f"hid_act{m}") for m in range(3)]
        hid_high = [sem(f"hid_high{m}") for m in range(3)]
        hid_split = [sem(f"hid_split{m}") for m in range(3)]
        hid_used = [sem(f"hid_used{m}") for m in range(3)]
        y_read = sem("y_read")
        y_done = sem("y_done")
        y_saved = [sem(f"y_saved{n}") for n in range(2)]

        block = ctx.enter_context(nc.Block())

        CONSTS = 9
        TURNS = (B - 6) // 2
        TURNS_2 = (B - 4) // 2

        def over_images(engine, step):
            for n in range(3):
                step(Image(engine, n, n % 2), True, True, n > 0)
            with engine.Fori(0, TURNS) as turn:
                step(Image(engine, engine.snap(turn * 2 + 3), 1), True, True, True)
                step(Image(engine, engine.snap(turn * 2 + 4), 0), True, True, True)
            step(Image(engine, B - 3, 1), True, True, True)
            step(Image(engine, B - 2, 0), False, True, True)
            step(Image(engine, B - 1, 1), False, False, True)

        def over_images_2(engine, step):
            step(Image(engine, 0, 0), True)
            step(Image(engine, 1, 1), True)
            with engine.Fori(0, TURNS_2) as turn:
                step(Image(engine, engine.snap(turn * 2 + 2), 0), True)
                step(Image(engine, engine.snap(turn * 2 + 3), 1), True)
            step(Image(engine, B - 2, 0), False)
            step(Image(engine, B - 1, 1), False)

        @block.sync
        def _(sp):
            def load_x(im, d):
                s = im.slot(d)
                wait(sp, rows_added, im.upto(d - 2))
                wait(sp, xcat_ready, im.upto(d - 2))
                n = im.index + d
                n = slice(n, n + 1) if isinstance(n, int) else bass.ds(n, 1)
                sp.dma_start(opp_x[s].rearrange("p a b c -> p (a b c)"),
                             opposite[n].rearrange("o p f -> (o p) f")).then_inc(x_in[s], 16)
                sp.dma_start(own_x[s], own[n].rearrange("o p c g -> (o p) (c g)")).then_inc(x_in[s], 16)

            def save(im):
                s = im.slot(-1)
                n = im.index - 1
                n = slice(n, n + 1) if isinstance(n, int) else bass.ds(n, 1)
                wait(sp, h1_ready, im.upto(-1))
                sp.dma_start(h1_dram[n].rearrange("o p f -> (o p) f"),
                             h1[s].rearrange("p a b -> p (a b)")).then_inc(h1_saved[s], 16)
                wait(sp, y2T_split, im.upto(-1))
                sp.dma_start(y2_dram[n].rearrange("o p f -> (o p) f"),
                             y2T[s].rearrange("p a b -> p (a b)")).then_inc(y2_saved[s], 16)

            zero = Image(sp, 0, 0)
            load_x(zero, 0)
            load_x(zero, 1)
            sp.dma_start(tok_raw, tokW).then_inc(weights_in, 16)
            sp.dma_start(tok_gam, tokGamma).then_inc(weights_in, 16)
            sp.dma_start(tok_bet, tokBeta).then_inc(weights_in, 16)
            sp.dma_start(tok_b, tokB.partition_broadcast(T)).then_inc(weights_in, 16)
            sp.dma_start(qkv_raw, qkvW).then_inc(weights_in, 16)
            sp.dma_start(proj_raw, projW).then_inc(weights_in, 16)
            sp.dma_start(gate_w, gateW).then_inc(weights_in, 16)
            load_x(zero, 2)

            def step(im, patches, prepare, project):
                if not isinstance(im.index, int) or im.index + 3 < B:
                    load_x(im, 3)
                if project:
                    save(im)

            over_images(sp, step)
            save(Image(sp, B, 0))
            for s in range(2):
                sp.wait_ge(h1_saved[s], 16 * (B // 2))
                sp.wait_ge(y2_saved[s], 16 * (B // 2))
            sp.wait_ge(gate_summed, B)
            sp.wait_ge(o_ready[2], B)
            for e in range(E):
                sp.dma_start(w1_raw[0:KC, e], W1[e].rearrange("(k p) f -> p k f", k=NKC)).then_inc(experts_in, 16)
                sp.dma_start(w2_raw[:, e], W2[e].rearrange("(c p) d -> p c d", c=FC)).then_inc(experts_in, 16)
            sp.dma_start(w1_raw[KC:KC + 1, :, NKC - 1, :], b1.rearrange("(o e) f -> o e f", o=1)).then_inc(experts_in, 16)
            sp.dma_start(b2_all, b2.rearrange("e d -> (e d)").partition_broadcast(T)).then_inc(experts_in, 16)

            def load_2(im, d):
                s = im.slot(d)
                n = im.index + d
                n = slice(n, n + 1) if isinstance(n, int) else bass.ds(n, 1)
                wait(sp, hid_ready[2], im.upto(d - 2))
                sp.dma_start(x2[s][0:KC].rearrange("p a k g -> p (a k g)"),
                             y2_dram[n].rearrange("o p f -> (o p) f")).then_inc(x2_in[s], 16)
                wait(sp, y_done, im.upto(d - 2))
                sp.dma_start(h1_in[s].rearrange("p a b -> p (a b)"),
                             h1_dram[n].rearrange("o p f -> (o p) f")).then_inc(h1_back[s], 16)

            zero = Image(sp, 0, 0)
            load_2(zero, 0)
            load_2(zero, 1)

            def step_2(im, more):
                s = im.parity
                wait(sp, y_done, im.upto(0))
                n = im.index
                n = slice(n, n + 1) if isinstance(n, int) else bass.ds(n, 1)
                sp.dma_start(out[n].rearrange("o (j p) d -> p (o j) d", j=2), y_fin[s]).then_inc(y_saved[s], 16)
                if more:
                    load_2(im, 2)

            over_images_2(sp, step_2)
            for s in range(2):
                sp.wait_ge(y_saved[s], 16 * (B // 2))

        @block.gpsimd
        def _(pool):
            pool.memset(ones, 1.0)
            pool.memset(eps_ln, EPS)
            pool.memset(minus_half, -0.5)
            pool.memset(ident, 0.0).then_inc(const_ready, 1)
            pool.memset(ident16, 0.0).then_inc(const_ready, 1)
            pool.wait_ge(const_ready, 2)
            for m in (ident, ident16):
                pool.affine_select(out=m, in_=m, compare_op=ALU.not_equal, fill=1.0, base=0,
                                   pattern=[[-1, 128]], channel_multiplier=1).then_inc(const_ready, 1)
            pool.memset(q_st, 0.0)
            pool.memset(k_st, 0.0)
            for s in range(2):
                pool.memset(val[s], 0.0).then_inc(const_ready, 1)
                pool.memset(q_even[s], 0.0)
                pool.memset(q_odd[s], 0.0)
            pool.wait_ge(const_ready, 6)
            for s in range(2):
                pool.memset(val[s][:, :, :, HD:HD + 1], 1.0).then_inc(const_ready, 1)
            pool.memset(tok_w[:, :, D:D + 1], 1.0).then_inc(const_ready, 1)

            def add_rows(im, d):
                s = im.slot(d)
                n = im.index + d
                if isinstance(n, int):
                    wait(pool, x_in[s], 32 * (n // 2 + 1))
                else:
                    pool.wait_ge(x_in[s], pool.snap((n - s) * 16 + 32))
                wait(pool, cols_added, im.upto(d - 1))
                pool.tensor_tensor(row_sum, opp_x[s][:, :, 0:SIDE, :], opp_x[s][:, :, 1:OPP, :],
                                   ALU.add).then_inc(rows_added, 1)

            def inverse_root(dst, shifted, src, eps, ready, step, done, im, d):
                wait(pool, ready, im.upto(d))
                pool.tensor_tensor(shifted, src, eps, ALU.add).then_inc(step, 1)
                wait(pool, step, im.upto(d))
                pool.tensor_tensor(dst, shifted, minus_half, ALU.pow).then_inc(done, 1)

            def root_tokens(im, d):
                inverse_root(tok_rstd, tok_sh, tok_var, eps_ln, tok_stat[2], tok_shifted, tok_stat[3], im, d)
                inverse_root(rstd1, sh1, mv1[:, :, 1], eps_ln, ln1_stat[1], ln1_shifted, ln1_stat[2], im, d)

            def root_h1(im):
                inverse_root(rstd2, sh2, mv2[:, :, 1], eps_ln, ln2_stat[1], ln2_shifted, ln2_stat[2], im, -1)

            def sum_squares(im, d):
                wait(pool, tok_ready, im.upto(d - 1))
                wait(pool, xsq_ready, im.upto(d))
                pool.tensor_tensor(xsq[:, 0:3], xsq[:, 0:3], xsq[:, 3:6], ALU.add).then_inc(xsq_fold[0], 1)
                wait(pool, xsq_fold[0], im.upto(d))
                pool.tensor_tensor(xsq[:, 0], xsq[:, 0], xsq[:, 1], ALU.add).then_inc(xsq_fold[1], 1)
                wait(pool, xsq_fold[1], im.upto(d))
                pool.tensor_tensor(xsq_sum, xsq[:, 0], xsq[:, 2], ALU.add).then_inc(xsq_summed, 1)

            def keep_h0(im, d):
                s = im.slot(d)
                n = im.index + d
                at = (n % 4) * 2 * D
                at = at if isinstance(n, int) else pool.snap(at)
                pool.wait_ge(const_ready, CONSTS)
                wait(pool, h1_ready, im.upto(d - 4))
                wait(pool, h0_ready, im.upto(d))
                pool.tensor_copy(h0_ring[:, bass.ds(at, 2 * D)] if not isinstance(at, int) else h0_ring[:, at:at + 2 * D],
                                 h0[s].rearrange("p a b -> p (a b)")).then_inc(h0_kept, 1)

            zero = Image(pool, 0, 0)
            add_rows(zero, 0)
            sum_squares(zero, 0)
            add_rows(zero, 1)
            root_tokens(zero, 0)
            sum_squares(zero, 1)
            keep_h0(zero, 0)
            root_tokens(zero, 1)

            def step(im, patches, prepare, project):
                if patches:
                    add_rows(im, 2)
                if prepare:
                    keep_h0(im, 1)
                if patches:
                    sum_squares(im, 2)
                if project:
                    root_h1(im)
                if patches:
                    root_tokens(im, 2)

            over_images(pool, step)
            root_h1(Image(pool, B, 0))

        @block.scalar
        def _(act):
            def square_x(im, d):
                s = im.slot(d)
                wait(act, xcat_ready, im.upto(d))
                wait(act, xsq_summed, im.upto(d - 1))
                act.activation(xsq, xcat[s], ACT.Square).then_inc(xsq_ready, 1)

            def high(psum, dst, ready, prev_used, done, im, d):
                wait(act, ready, im.upto(d))
                for sem_, n in prev_used:
                    wait(act, sem_, n)
                act.activation(dst[:, 0], psum[0:KC, 0:NKC * G], ACT.Copy, scale=S_ACT).then_inc(done, 1)

            def high_y(im, d):
                high(X, yT, yT_ready, [(qkv_ready[1], im.upto(d - 1))], yT_high, im, d)

            def square_qk(im, d, j):
                wait(act, qkv_ready[j], im.upto(d))
                wait(act, qk_summed, im.upto(d - 1))
                act.activation(qk_sq[:, j], (Y, Z)[j][0:T, 0:2 * D], ACT.Square).then_inc(qk_squared[j], 1)

            def high_qk(im, d):
                wait(act, qk_normed, im.upto(d))
                wait(act, stack_T[1], im.upto(d - 1))
                for n, (dst, blocks) in enumerate(((q_st, slice(0, 3, 2)), (k_st, slice(0, 2)))):
                    last = act.activation(
                        dst.rearrange("p h (b e) -> p h b e", b=4)[:, :, blocks, :],
                        qk_n[:, n].unsqueeze(2).to_broadcast([T, 2 * HEADS, 2, HD]), ACT.Copy, scale=S_QK)
                last.then_inc(qk_high, 1)

            def values(im, d):
                s = im.slot(d)
                wait(act, qkv_ready[1], im.upto(d))
                wait(act, o_ready[2], im.upto(d - 2))
                act.activation(val[s][:, :, :, 0:HD].rearrange("p k h e -> p (k h) e"),
                               X[0:T, 0:2 * D].rearrange("p (h e) -> p h e", e=HD),
                               ACT.Copy, scale=1.0 / (S_ACT * S_W)).then_inc(v_ready, 1)

            def keys(im, d, r):
                s = im.slot(d)
                wait(act, stack_T[r], im.upto(d))
                wait(act, scores_ready[HEADS - 1], im.upto(d - 2))
                act.copy(kT[s][:, 3 * r:3 * r + 3, :].rearrange("p h g -> p (h g)"),
                         X16[:, 0:3 * G]).then_inc(k_ready[r], 1)

            def exps(im, h):
                wait(act, scores_ready[h], im.upto(0))
                wait(act, o_ready[h // 4], im.upto(-1))
                act.activation(prob[h], S[h % 3][0:T, 0:2 * G], ACT.Exp,
                               scale=HD ** 0.5 / (S_QK * S_QK)).then_inc(prob_ready[h], 1)

            def o_copy(im, d, g):
                wait(act, o_ready[g], im.upto(d))
                wait(act, o_tokens, im.upto(d - 1))
                act.copy(oT[:, g, :], o_bank(im.slot(d), g)[:, 0:G]).then_inc(o_out[g], 1)

            def high_a(im):
                high(X, aT, aT_ready, [(proj_ready, im.upto(-2))], aT_high, im, -1)

            def high_y2(im):
                n = im.index - 1
                s = im.slot(-1)
                if isinstance(n, int):
                    prev = [(y2_saved[s], 16 * (n // 2))]
                else:
                    prev = [(y2_saved[s], act.snap((n - s) * 8))]
                high(Z, y2T[s], y2T_ready, prev, y2T_high, im, -1)

            act.wait_ge(weights_ready, 1)
            zero = Image(act, 0, 0)
            square_x(zero, 0)
            square_x(zero, 1)
            high_y(zero, 0)
            square_qk(zero, 0, 0)
            square_qk(zero, 0, 1)
            values(zero, 0)
            high_qk(zero, 0)
            keys(zero, 0, 0)
            keys(zero, 0, 1)

            def step(im, patches, prepare, project):
                exps(im, 0)
                exps(im, 1)
                if prepare:
                    high_y(im, 1)
                if project:
                    o_copy(im, -1, 2)
                exps(im, 2)
                exps(im, 3)
                if prepare:
                    square_qk(im, 1, 0)
                    square_qk(im, 1, 1)
                    values(im, 1)
                exps(im, 4)
                exps(im, 5)
                if prepare:
                    high_qk(im, 1)
                if patches:
                    square_x(im, 2)
                o_copy(im, 0, 0)
                if project:
                    high_a(im)
                exps(im, 6)
                exps(im, 7)
                exps(im, 8)
                o_copy(im, 0, 1)
                if prepare:
                    keys(im, 1, 0)
                exps(im, 9)
                if prepare:
                    keys(im, 1, 1)
                exps(im, 10)
                exps(im, 11)
                if project:
                    high_y2(im)

            over_images(act, step)
            last = Image(act, B, 0)
            o_copy(last, -1, 2)
            high_a(last)
            high_y2(last)

            act.wait_ge(gate_step, 3)
            act.activation(g_exp, g_sub, ACT.Exp).then_inc(gate_exp, 1)

            def hidden(im, d):
                for m in range(3):
                    wait(act, hid_ready[m], im.upto(d))
                    wait(act, hid_split[m], im.upto(d - 1))
                    act.activation(hid[m], bank[m][:, 0:2 * G], ACT.Gelu,
                                   scale=1.0 / (S_ACT * S_W)).then_inc(hid_act[m], 1)
                    wait(act, hid_act[m], im.upto(d))
                    wait(act, hid_used[m], im.upto(d - 1))
                    act.activation(hidT[m][:, 0], hid[m], ACT.Copy, scale=S_HID).then_inc(hid_high[m], 1)

            hidden(Image(act, 0, 0), 0)

            def step_2(im, more):
                if more or im.index + 1 < B:
                    hidden(im, 1)

            over_images_2(act, step_2)

        @block.vector
        def _(dve):
            done = [0]

            def self_step(ins):
                done[0] += 1
                ins.then_inc(setup_dve, 1)
                dve.wait_ge(setup_dve, done[0])

            dve.wait_ge(weights_in, 16 * 7)
            dve.wait_ge(const_ready, CONSTS)
            self_step(dve.tensor_tensor(tok_w[:, :, 0:D], tok_raw,
                                        tok_gam.unsqueeze(2).to_broadcast([128, CB, D]), ALU.mult))
            self_step(dve.tensor_copy(beta_cols, tok_bet.unsqueeze(2).to_broadcast([128, CB, T])))
            self_step(dve.tensor_reduce(qkv_gs, qkv_raw[:, :, 0:2 * D].rearrange("p k (g e) -> p k g e", e=HD),
                                        AX_X, ALU.add))
            for k in range(NKC):
                self_step(dve.scalar_tensor_tensor(
                    qkv_raw[:, k, 0:2 * D].rearrange("p (g e) -> p g e", e=HD),
                    qkv_gs[:, k].unsqueeze(2).to_broadcast([KC, 2 * HEADS, HD]), -1.0 / HD,
                    qkv_raw[:, k, 0:2 * D].rearrange("p (g e) -> p g e", e=HD), ALU.mult, ALU.add))
            self_step(dve.tensor_scalar(qkv_w[:, 0], qkv_raw, S_W, None, ALU.mult))
            self_step(dve.scalar_tensor_tensor(qkv_w[:, 1], qkv_raw, S_W, qkv_w[:, 0], ALU.mult, ALU.subtract))
            self_step(dve.tensor_scalar(proj_w[:, 0], proj_raw, S_W, None, ALU.mult))
            self_step(dve.scalar_tensor_tensor(proj_w[:, 1], proj_raw, S_W, proj_w[:, 0], ALU.mult, ALU.subtract))
            dve.wait_ge(setup_mm, 1)
            self_step(dve.scalar_tensor_tensor(
                tok_w[:, :, 0:D], X[:, 0:D].unsqueeze(1).to_broadcast([128, CB, D]), -1.0 / PD,
                tok_w[:, :, 0:D], ALU.mult, ALU.add))
            dve.tensor_tensor(tok_bias, Y[0:T, 0:D], tok_b, ALU.add).then_inc(weights_ready, 1)

            def add_cols(im, d):
                s = im.slot(d)
                wait(dve, rows_added, im.upto(d))
                wait(dve, tok_ready, im.upto(d - 2))
                wait(dve, xsq_ready, im.upto(d - 2))
                rows = row_sum.rearrange("p c r q -> p (c r) q")
                dve.tensor_tensor(xcat[s].rearrange("p c (r q) -> p (c r) q", q=SIDE),
                                  rows[:, :, 0:SIDE], rows[:, :, 1:OPP], ALU.add).then_inc(cols_added, 1)
                wait(dve, cols_added, im.upto(d))
                flat = xcat[s].rearrange("p c g -> p (c g)")
                dve.tensor_tensor(flat, flat, own_x[s], ALU.add).then_inc(xcat_ready, 1)

            def normalise(src, src_ready, dst, bn, mv, rstd, steps, dst_ready, im, d):
                wait(dve, src_ready, im.upto(d))
                for j in range(2):
                    last = dve.bn_stats(bn[:, j], src[:, j])
                last.then_inc(steps[0], 1)
                dve.wait_ge(weights_ready, 1)
                wait(dve, steps[0], im.upto(d))
                for j in range(2):
                    last = dve.bn_aggr(mv[:, j], bn[:, j])
                last.then_inc(steps[1], 1)
                wait(dve, steps[2], im.upto(d))
                for j in range(2):
                    last = dve.tensor_scalar(dst[:, j], src[:, j], mv[:, j, 0:1], rstd[:, j:j + 1],
                                             ALU.subtract, ALU.mult)
                last.then_inc(dst_ready, 1)

            def tokens(im, d):
                s = im.slot(d)
                wait(dve, tok_ready, im.upto(d))
                dve.tensor_scalar(tok_mean, Y[0:T, D:2 * (D + 1):D + 1], 1.0 / PD, None,
                                  ALU.mult).then_inc(tok_stat[0], 1)
                wait(dve, tok_stat[0], im.upto(d))
                dve.tensor_tensor(tok_mean2, tok_mean, tok_mean, ALU.mult).then_inc(tok_stat[1], 1)
                wait(dve, tok_stat[1], im.upto(d))
                dve.scalar_tensor_tensor(tok_var, Y[0:T, 2 * (D + 1):2 * (D + 1) + 2], 1.0 / PD, tok_mean2,
                                         ALU.mult, ALU.subtract).then_inc(tok_stat[2], 1)
                wait(dve, tok_stat[3], im.upto(d))
                wait(dve, h0_kept, im.upto(d - 2))
                for j in range(2):
                    last = dve.scalar_tensor_tensor(h0[s][:, j], Y[0:T, j * (D + 1):j * (D + 1) + D],
                                                    tok_rstd[:, j:j + 1], tok_bias, ALU.mult, ALU.add)
                last.then_inc(h0_ready, 1)
                wait(dve, yT_ready, im.upto(d - 1))
                normalise(h0[s], h0_ready, y, bn1, mv1, rstd1, ln1_stat, y_ready, im, d)

            def low(psum, dst, high_done, split, im, d):
                wait(dve, high_done, im.upto(d))
                dve.scalar_tensor_tensor(dst[:, 1], psum[0:KC, 0:NKC * G], S_ACT, dst[:, 0],
                                         ALU.mult, ALU.subtract).then_inc(split, 1)

            def norm_qk(im, d):
                wait(dve, qk_squared[0], im.upto(d))
                wait(dve, qk_squared[1], im.upto(d))
                dve.tensor_reduce(qk_ss, qk_sq.rearrange("p j (h e) -> p (j h) e", e=HD), AX_X,
                                  ALU.add).then_inc(qk_summed, 1)
                wait(dve, qk_summed, im.upto(d))
                dve.tensor_scalar(qk_var, qk_ss, EPS_QK, None, ALU.add).then_inc(qk_step[0], 1)
                wait(dve, qk_step[0], im.upto(d))
                dve.tensor_scalar(qk_rs.bitcast(I32), qk_var.bitcast(I32), -0.5, float(0x5F3759DF),
                                  ALU.mult, ALU.add).then_inc(qk_step[1], 1)
                for n in range(NEWTON):
                    wait(dve, qk_step[3 * n + 1], im.upto(d))
                    dve.scalar_tensor_tensor(qk_t, qk_rs, -0.5, qk_rs, ALU.mult, ALU.mult).then_inc(qk_step[3 * n + 2], 1)
                    wait(dve, qk_step[3 * n + 2], im.upto(d))
                    dve.tensor_tensor(qk_t, qk_t, qk_var, ALU.mult).then_inc(qk_step[3 * n + 3], 1)
                    wait(dve, qk_step[3 * n + 3], im.upto(d))
                    dve.scalar_tensor_tensor(qk_rs, qk_t, 1.5, qk_rs, ALU.add, ALU.mult).then_inc(qk_step[3 * n + 4], 1)
                wait(dve, qk_step[3 * NEWTON + 1], im.upto(d))
                wait(dve, qk_high, im.upto(d - 1))
                for j in range(2):
                    rs = qk_rs[:, j * 2 * HEADS:(j + 1) * 2 * HEADS].rearrange("p (a h) -> p a h", a=2)
                    last = dve.tensor_tensor(
                        qk_n[:, :, j * HEADS:(j + 1) * HEADS, :],
                        (Y, Z)[j][0:T, 0:2 * D].rearrange("p (a h e) -> p a h e", a=2, e=HD),
                        rs.unsqueeze(3).to_broadcast([T, 2, HEADS, HD]), ALU.mult)
                last.then_inc(qk_normed, 1)

            def low_qk(im, d):
                wait(dve, qk_high, im.upto(d))
                dve.scalar_tensor_tensor(q_st[:, :, HD:2 * HD], qk_n[:, 0], S_QK, q_st[:, :, 0:HD],
                                         ALU.mult, ALU.subtract)
                dve.scalar_tensor_tensor(k_st[:, :, 2 * HD:3 * HD], qk_n[:, 1], S_QK, k_st[:, :, 0:HD],
                                         ALU.mult, ALU.subtract).then_inc(qk_split, 1)

            def queries(im, d, r):
                s = im.slot(d)
                wait(dve, stack_T[r], im.upto(d))
                wait(dve, scores_ready[HEADS - 1], im.upto(d - 2))
                for dst, lo in ((q_even[s], 0), (q_odd[s], 64)):
                    last = dve.tensor_copy(dst[lo:lo + 64, 3 * r:3 * r + 3, :].rearrange("p h g -> p (h g)"),
                                           Z16[lo:lo + 64, 0:3 * G])
                last.then_inc(q_ready[r], 1)

            def norm_attn(im):
                wait(dve, o_tokens, im.upto(-1))
                wait(dve, aT_ready, im.upto(-2))
                src = [t[0:T, 0:3 * 128].rearrange("p (h w) -> p h w", w=HW)
                       for t in (X, o_bank(im.slot(-1), 2))]
                for j in range(2):
                    last = dve.reciprocal(rden[:, j], src[j][:, :, HD])
                last.then_inc(den_inv, 1)
                wait(dve, den_inv, im.upto(-1))
                for j in range(2):
                    last = dve.tensor_tensor(attn[:, j].rearrange("p (h e) -> p h e", e=HD), src[j][:, :, 0:HD],
                                             rden[:, j].unsqueeze(2).to_broadcast([T, HEADS, HD]), ALU.mult)
                last.then_inc(attn_ready, 1)

            def residual(im):
                s = im.slot(-1)
                n = im.index - 1
                at = n % 4 * 2 * D
                if isinstance(n, int):
                    kept = h0_ring[:, at:at + 2 * D]
                    wait(dve, h1_saved[s], 16 * (n // 2))
                else:
                    kept = h0_ring[:, bass.ds(dve.snap(at), 2 * D)]
                    dve.wait_ge(h1_saved[s], dve.snap((n - s) * 8))
                wait(dve, proj_ready, im.upto(-1))
                dve.scalar_tensor_tensor(h1[s].rearrange("p a b -> p (a b)"), X[0:T, 0:2 * D], 1.0 / (S_ACT * S_W),
                                         kept, ALU.mult, ALU.add).then_inc(h1_ready, 1)
                wait(dve, y2T_ready, im.upto(-2))
                normalise(h1[s], h1_ready, y2, bn2, mv2, rstd2, ln2_stat, y2_ready, im, -1)

            def gate_sums(im):
                n = im.index - 1
                at = n if isinstance(n, int) else dve.snap(n)
                dst = gate_sum[:, at, :] if isinstance(n, int) else gate_sum[:, bass.ds(at, 1), :].rearrange("p o k -> p (o k)")
                dve.tensor_reduce(dst, Z[0:KC, 0:NKC * G].rearrange("p (k g) -> p k g", g=G), AX_X,
                                  ALU.add).then_inc(gate_summed, 1)

            zero = Image(dve, 0, 0)
            add_cols(zero, 0)
            add_cols(zero, 1)
            dve.wait_ge(weights_ready, 1)
            tokens(zero, 0)
            low(X, yT, yT_high, yT_split, zero, 0)
            norm_qk(zero, 0)
            low_qk(zero, 0)
            queries(zero, 0, 0)
            queries(zero, 0, 1)
            tokens(zero, 1)

            def step(im, patches, prepare, project):
                if prepare:
                    low(X, yT, yT_high, yT_split, im, 1)
                if patches:
                    add_cols(im, 2)
                if prepare:
                    norm_qk(im, 1)
                if project:
                    norm_attn(im)
                if prepare:
                    low_qk(im, 1)
                if project:
                    low(X, aT, aT_high, aT_split, im, -1)
                    residual(im)
                if prepare:
                    queries(im, 1, 0)
                    queries(im, 1, 1)
                if patches:
                    tokens(im, 2)
                if project:
                    low(Z, y2T[im.slot(-1)], y2T_high, y2T_split, im, -1)
                    gate_sums(im)

            over_images(dve, step)
            last = Image(dve, B, 0)
            norm_attn(last)
            low(X, aT, aT_high, aT_split, last, -1)
            residual(last)
            low(Z, y2T[last.slot(-1)], y2T_high, y2T_split, last, -1)
            gate_sums(last)

            dve.wait_ge(h1_saved[1], 16 * (B // 2))
            dve.wait_ge(o_ready[2], B)
            dve.wait_ge(aT_ready, B)
            dve.wait_ge(gate_summed, B)
            dve.memset(w1_raw[KC:KC + 1, :, 0, :], 0.0)
            for s in range(2):
                dve.memset(x2[s][KC:KC + 1], 0.0).then_inc(rows_set, 1)
            dve.wait_ge(rows_set, 2)
            for s in range(2):
                dve.memset(x2[s][KC:KC + 1, 0, NKC - 1], S_ACT).then_inc(rows_set, 1)
            gates = [0]

            def gate_do(ins):
                gates[0] += 1
                ins.then_inc(gate_step, 1)
                dve.wait_ge(gate_step, gates[0])

            dve.wait_ge(logits_ready, 1)
            gate_do(dve.tensor_scalar(g_logit, X[0:B, 0:E], 1.0 / G, None, ALU.mult))
            gate_do(dve.tensor_reduce(g_max, g_logit, AX_X, ALU.max))
            gate_do(dve.tensor_scalar(g_sub, g_logit, g_max[:, 0:1], None, ALU.subtract))
            gate_do(dve.tensor_scalar(g_is, g_sub, 0.0, None, ALU.is_ge))
            for n in range(2):
                gate_do(dve.tensor_scalar(g_not[:, n:n + 1], g_is[:, n:n + 1], -1.0, float(n + 1), ALU.mult, ALU.add))
            gate_do(dve.tensor_tensor(g_pair[:, 1:2], g_not[:, 0:1], g_not[:, 1:2], ALU.mult))
            dve.wait_ge(gate_exp, 1)
            gate_do(dve.tensor_reduce(g_sum, g_exp, AX_X, ALU.add))
            gate_do(dve.reciprocal(g_pair[:, 0:1], g_sum))
            dve.tensor_copy(g_wide, g_pair.unsqueeze(2).to_broadcast([B, 2, T])).then_inc(gate_wide, 1)
            dve.wait_ge(gate_ready, 1)
            gate_do(dve.tensor_copy(gate, Y[0:T, 0:B]))
            gate_do(dve.tensor_copy(expert_f, Y[0:1, B:2 * B]))
            dve.tensor_copy(expert, expert_f).then_inc(expert_known, 1)
            dve.wait_ge(expert_known, 1)

            dve.wait_ge(experts_in, 16 * (2 * E + 2))
            w1_v = w1_all.rearrange("p (e a n) -> p e a n", e=E, a=2)
            w2_v = w2_all.rearrange("p (e a n) -> p e a n", e=E, a=2)
            for v, raw in ((w1_v, w1_raw.rearrange("p e k f -> p e (k f)")), (w2_v, w2_raw.rearrange("p e c d -> p e (c d)"))):
                gate_do(dve.tensor_scalar(v[:, :, 0], raw, S_W, None, ALU.mult))
                gate_do(dve.scalar_tensor_tensor(v[:, :, 1], raw, S_W, v[:, :, 0], ALU.mult, ALU.subtract))

            N1, N2 = 2 * NKC * FF, 2 * FC * D

            def expert_of(im, d):
                n = im.index + d
                at = expert[0:1, n:n + 1] if isinstance(n, int) else expert[0:1, bass.ds(n, 1)]
                return dve.value_load(at, min_val=0, max_val=E - 1)

            def choose_w1(im, d, e):
                s = im.slot(d)
                wait(dve, hid_ready[2], im.upto(d - 2))
                dve.tensor_copy(w1_sel[s].rearrange("p a k f -> p (a k f)"),
                                w1_all[:, bass.ds(dve.snap(e * N1), N1)]).then_inc(w1_chosen, 1)

            def choose_w2(im, d, e):
                s = im.slot(d)
                wait(dve, hid_used[2], im.upto(d - 2))
                dve.tensor_copy(w2_sel[s].rearrange("p a c d -> p (a c d)"),
                                w2_all[:, bass.ds(dve.snap(e * N2), N2)]).then_inc(w2_chosen, 1)

            def low_hidden(im, d):
                for m in range(3):
                    wait(dve, hid_high[m], im.upto(d))
                    dve.scalar_tensor_tensor(hidT[m][:, 1], hid[m], S_HID, hidT[m][:, 0],
                                             ALU.mult, ALU.subtract).then_inc(hid_split[m], 1)

            def finish(im, e):
                s = im.parity
                n = im.index
                bias = b2_all[:, bass.ds(dve.snap(e * D), D)]
                wait(dve, hid_used[2], im.upto(0))
                for j in range(2):
                    last = dve.scalar_tensor_tensor(y_out[s][:, j], bank[3 + 2 * s + j][0:T, 0:D], 1.0 / (S_HID * S_W),
                                                    bias, ALU.mult, ALU.add)
                last.then_inc(y_read, 1)
                if isinstance(n, int):
                    wait(dve, h1_back[s], 16 * (n // 2 + 1))
                    wait(dve, y_saved[s], 16 * (n // 2))
                else:
                    dve.wait_ge(h1_back[s], dve.snap((n - s) * 8 + 16))
                    dve.wait_ge(y_saved[s], dve.snap((n - s) * 8))
                wait(dve, y_read, im.upto(0))
                g = gate[:, n:n + 1] if isinstance(n, int) else gate[:, bass.ds(n, 1)]
                dve.scalar_tensor_tensor(y_fin[s], y_out[s], g, h1_in[s], ALU.mult, ALU.add).then_inc(y_done, 1)

            zero = Image(dve, 0, 0)
            for d in range(2):
                e = expert_of(zero, d)
                choose_w1(zero, d, e)
                choose_w2(zero, d, e)
            low_hidden(zero, 0)

            def step_2(im, more):
                if more:
                    ahead = expert_of(im, 2)
                    choose_w1(im, 2, ahead)
                if more or im.index + 1 < B:
                    low_hidden(im, 1)
                finish(im, expert_of(im, 0))
                if more:
                    choose_w2(im, 2, ahead)

            over_images_2(dve, step_2)

        @block.tensor
        def _(pe):
            def split_product(dst, left, right, cols, groups, start_first=True):
                pairs = [(a, b, k) for a, b in ((0, 0), (0, 1), (1, 0)) for k in range(groups)]
                for n, (a, b, k) in enumerate(pairs):
                    last = pe.matmul(dst, left(a, k), right(b, k)[:, cols], start=(n == 0), stop=(n == len(pairs) - 1))
                return last

            pe.wait_ge(const_ready, CONSTS)
            pe.wait_ge(setup_dve, 2)
            for c in range(CB):
                pe.matmul(X[:, 0:D], ones[:, :], tok_w[:, c, 0:D], start=(c == 0), stop=(c == CB - 1))
            for c in range(CB):
                last = pe.matmul(Y[0:T, 0:D], beta_cols[:, c], tok_raw[:, c], start=(c == 0), stop=(c == CB - 1))
            last.then_inc(setup_mm, 1)

            def patches_mm(im, d, j):
                s = im.slot(d)
                if j == 0:
                    wait(pe, xcat_ready, im.upto(d))
                    wait(pe, qk_normed, im.upto(d - 1))
                    wait(pe, h0_ready, im.upto(d - 1))
                for c in range(CB):
                    pe.matmul(Y[0:T, j * (D + 1):(j + 1) * (D + 1)], xcat[s][:, c, j * T:(j + 1) * T], tok_w[:, c],
                              start=(c == 0), stop=(c == CB - 1))
                if j == 1:
                    wait(pe, xsq_summed, im.upto(d))
                    for jj in range(2):
                        last = pe.matmul(Y[0:T, 2 * (D + 1) + jj:2 * (D + 1) + jj + 1],
                                         xsq_sum[:, jj * T:(jj + 1) * T], ones[:, 0:1], start=True, stop=True)
                    last.then_inc(tok_ready, 1)

            def turn(dst, src, done):
                for k in range(NKC):
                    for j in range(2):
                        last = pe.transpose(dst[0:KC, k * G + j * T:k * G + (j + 1) * T],
                                            src[:, j, k * KC:(k + 1) * KC], ident[0:T, 0:T])
                last.then_inc(done, 1)

            def turn_y(im, d):
                wait(pe, y_ready, im.upto(d))
                wait(pe, k_ready[1], im.upto(d - 1))
                turn(X, y, yT_ready)

            def qkv(im, d, j):
                if j == 0:
                    wait(pe, yT_split, im.upto(d))
                else:
                    wait(pe, gate_summed, im.upto(d - 3))
                left = lambda a, k: yT[:, a, k * G + j * T:k * G + (j + 1) * T]
                right = lambda b, k: qkv_w[:, b, k]
                split_product((Y, Z)[j][0:T, 0:2 * D], left, right, slice(0, 2 * D), NKC)
                split_product(X[0:T, j * D:(j + 1) * D], left, right, slice(2 * D, 3 * D), NKC)\
                    .then_inc(qkv_ready[j], 1)

            def turn_qk(im, d, r):
                if r == 0:
                    wait(pe, qk_split, im.upto(d))
                    wait(pe, v_ready, im.upto(d))
                    wait(pe, h1_ready, im.upto(d - 2))
                else:
                    wait(pe, q_ready[0], im.upto(d))
                    wait(pe, k_ready[0], im.upto(d))
                for p in range(3):
                    for j in range(2):
                        h = j * HEADS + 2 * (3 * r + p)
                        at = slice(p * G + j * T, p * G + (j + 1) * T)
                        for dst, st in ((Z16, q_st), (X16, k_st)):
                            last = pe.transpose(dst[:, at], st[:, h:h + 2, :].rearrange("p h e -> p (h e)"),
                                                ident16[0:T, 0:T])
                last.then_inc(stack_T[r], 1)

            def scores(im, h):
                s = im.parity
                if h % 6 == 0:
                    wait(pe, q_ready[h // 6], im.upto(0))
                    wait(pe, k_ready[h // 6], im.upto(0))
                wait(pe, prob_ready[(h - 3) % HEADS], im.upto(0 if h >= 3 else -1))
                q = (q_even, q_odd)[h % 2][s]
                for k in range(2):
                    last = pe.matmul(S[h % 3][0:T, k * G:(k + 1) * G], kT[s][:, h // 2, k * T:(k + 1) * T],
                                     q[:, h // 2, :], start=True, stop=True)
                last.then_inc(scores_ready[h], 1)

            def weigh(im, d, g):
                s = im.slot(d)
                wait(pe, prob_ready[4 * g + 3], im.upto(d))
                wait(pe, v_ready, im.upto(d))
                if g == 2:
                    wait(pe, o_out[0], im.upto(d))
                elif g == 0:
                    wait(pe, o_out[1], im.upto(d - 1))
                else:
                    wait(pe, o_out[2], im.upto(d - 1))
                    wait(pe, attn_ready, im.upto(d - 1))
                dst = o_bank(s, g)
                for k in range(2):
                    for q in range(4):
                        h = 4 * g + q
                        last = pe.matmul(dst[HW * q:HW * (q + 1), 0:G], val[s][:, k, h], prob[h][:, k * G:(k + 1) * G],
                                         start=(k == 0), stop=(k == 1))
                last.then_inc(o_ready[g], 1)

            def turn_o(im):
                wait(pe, o_out[2], im.upto(-1))
                if im.has_next:
                    wait(pe, v_ready, im.upto(1))
                else:
                    wait(pe, k_ready[1], B)
                    wait(pe, h1_ready, im.upto(-2))
                for j, dst in enumerate((X, o_bank(im.slot(-1), 2))):
                    for g in range(3):
                        last = pe.transpose(dst[0:T, g * 128:(g + 1) * 128], oT[:, g, j * T:(j + 1) * T], ident[:, :])
                last.then_inc(o_tokens, 1)

            def turn_a(im):
                wait(pe, attn_ready, im.upto(-1))
                turn(X, attn, aT_ready)

            def project_mm(im):
                wait(pe, aT_split, im.upto(-1))
                for j in range(2):
                    last = split_product(X[0:T, j * D:(j + 1) * D],
                                         lambda a, k: aT[:, a, k * G + j * T:k * G + (j + 1) * T],
                                         lambda b, k: proj_w[:, b, k], slice(0, D), NKC)
                last.then_inc(proj_ready, 1)

            def turn_y2(im):
                wait(pe, y2_ready, im.upto(-1))
                if im.has_next:
                    wait(pe, q_ready[1], im.upto(1))
                else:
                    wait(pe, gate_summed, im.upto(-2))
                turn(Z, y2, y2T_ready)

            pe.wait_ge(weights_ready, 1)
            zero = Image(pe, 0, 0)
            patches_mm(zero, 0, 0)
            patches_mm(zero, 0, 1)
            turn_y(zero, 0)
            qkv(zero, 0, 0)
            qkv(zero, 0, 1)
            turn_qk(zero, 0, 0)
            turn_qk(zero, 0, 1)
            patches_mm(zero, 1, 0)
            patches_mm(zero, 1, 1)

            def step(im, patches, prepare, project):
                im.has_next = prepare
                scores(im, 0)
                scores(im, 1)
                if prepare:
                    turn_y(im, 1)
                if project:
                    weigh(im, -1, 2)
                scores(im, 2)
                if prepare:
                    qkv(im, 1, 0)
                scores(im, 3)
                if prepare:
                    qkv(im, 1, 1)
                if project:
                    turn_o(im)
                scores(im, 4)
                weigh(im, 0, 0)
                scores(im, 5)
                if project:
                    turn_a(im)
                if patches:
                    patches_mm(im, 2, 0)
                scores(im, 6)
                if project:
                    project_mm(im)
                scores(im, 7)
                if patches:
                    patches_mm(im, 2, 1)
                scores(im, 8)
                weigh(im, 0, 1)
                if prepare:
                    turn_qk(im, 1, 0)
                scores(im, 9)
                if prepare:
                    turn_qk(im, 1, 1)
                scores(im, 10)
                scores(im, 11)
                if project:
                    turn_y2(im)

            over_images(pe, step)
            last = Image(pe, B, 0)
            last.has_next = False
            weigh(last, -1, 2)
            for f in (turn_o, turn_a, project_mm, turn_y2):
                f(last)

            pe.wait_ge(gate_summed, B)
            pe.wait_ge(h1_ready, B)
            for k in range(NKC):
                last = pe.matmul(X[0:B, 0:E], gate_sum[:, :, k], gate_w[:, k], start=(k == 0), stop=(k == NKC - 1))
            last.then_inc(logits_ready, 1)
            pe.wait_ge(gate_wide, 1)
            for n in range(2):
                last = pe.matmul(Y[0:T, n * B:(n + 1) * B], g_wide[:, n], ident[0:B, 0:B], start=True, stop=True)
            last.then_inc(gate_ready, 1)

            def first_product(im, d, m):
                s = im.slot(d)
                n = im.index + d
                if m == 0:
                    wait(pe, w1_chosen, im.upto(d))
                    if isinstance(n, int):
                        wait(pe, x2_in[s], 16 * (n // 2 + 1))
                    else:
                        pe.wait_ge(x2_in[s], pe.snap((n - s) * 8 + 16))
                wait(pe, hid_act[m], im.upto(d - 1))
                for c in range(2):
                    f = (2 * m + c) * 128
                    rows = lambda k: KC + (k == NKC - 1)
                    last = split_product(bank[m][:, c * G:(c + 1) * G],
                                         lambda a, k: w1_sel[s][0:rows(k), a, k, f:f + 128],
                                         lambda b, k: x2[s][0:rows(k), b, k], slice(0, G), NKC)
                last.then_inc(hid_ready[m], 1)

            def second_product(im, m):
                s = im.parity
                wait(pe, hid_split[m], im.upto(0))
                if m == 0:
                    wait(pe, w2_chosen, im.upto(0))
                    wait(pe, y_read, im.upto(-2))
                for c in range(2):
                    for j in range(2):
                        for n, (a, b) in enumerate(((0, 0), (0, 1), (1, 0))):
                            last = pe.matmul(bank[3 + 2 * s + j][0:T, 0:D],
                                             hidT[m][:, a, c * G + j * T:c * G + (j + 1) * T],
                                             w2_sel[s][:, b, 2 * m + c],
                                             start=(m == 0 and c == 0 and n == 0), stop=(m == 2 and c == 1 and n == 2))
                last.then_inc(hid_used[m], 1)

            zero = Image(pe, 0, 0)
            pe.wait_ge(rows_set, 4)
            pe.wait_ge(expert_known, 1)
            for m in range(3):
                first_product(zero, 0, m)

            def step_2(im, more):
                for m in range(3):
                    if more or im.index + 1 < B:
                        first_product(im, 1, m)
                    second_product(im, m)

            over_images_2(pe, step_2)



def kernel(x, L0_tok_gamma, L0_tok_beta, L0_tok_W, L0_tok_b, L0_attn_qkv_weight, L0_attn_proj_weight,
           L0_ffn_Wg, L0_ffn_W1, L0_ffn_b1, L0_ffn_W2, L0_ffn_b2):
    import numpy as np
    import concourse.bacc as bacc
    from concourse.bass_utils import run_bass_kernel_spmd

    x = np.asarray(x)
    B, C, H, W = x.shape
    R = H // PATCH
    parts = x.reshape(B, C, R, 2, HALF, R, 2, HALF).transpose(3, 6, 0, 4, 7, 1, 2, 5)
    own = np.ascontiguousarray(parts.transpose(2, 0, 3, 4, 5, 1, 6, 7)).reshape(B, 128, CH * 2, R * R)
    opposite = np.zeros((B, 2, HALF, HALF, C, 2, R + 1, R + 1), x.dtype)
    for a in range(2):
        for b in range(2):
            opposite[:, a, :, :, :, b, 1 - a:1 - a + R, 1 - b:1 - b + R] = parts[1 - a, 1 - b]
    opposite = opposite.reshape(B, 128, CH * 2 * (R + 1) * (R + 1))

    def by_pixel(v):
        v = np.asarray(v).reshape(-1, 2, HALF, 2, HALF, CH)
        return np.ascontiguousarray(v.transpose(1, 2, 4, 5, 3, 0)).reshape(128, CH * 2, -1)

    def by_chunk(v):
        v = np.asarray(v).T
        return np.ascontiguousarray(v.reshape(NKC, KC, -1).transpose(1, 0, 2))

    arrays = {
        "own": own, "opposite": opposite, "tok_W": by_pixel(L0_tok_W),
        "tok_gamma": by_pixel(L0_tok_gamma)[:, :, 0], "tok_beta": by_pixel(L0_tok_beta)[:, :, 0],
        "tok_b": np.asarray(L0_tok_b), "qkv_W": by_chunk(L0_attn_qkv_weight), "proj_W": by_chunk(L0_attn_proj_weight),
        "gate_W": by_chunk(L0_ffn_Wg), "W1": np.asarray(L0_ffn_W1), "b1": np.asarray(L0_ffn_b1),
        "W2": np.asarray(L0_ffn_W2), "b2": np.asarray(L0_ffn_b2),
    }
    arrays = {k: np.ascontiguousarray(v) for k, v in arrays.items()}
    nc = bacc.Bacc("TRN2", target_bir_lowering=False, num_devices=1, dynamic_dma_scratch_size=1024)
    args = [nc.dram_tensor(f"in_{k}", v.shape, mybir.dt.from_np(v.dtype), kind="ExternalInput").ap()
            for k, v in arrays.items()]
    out = nc.dram_tensor("out_0", (B, R * R, D), F32, kind="ExternalOutput").ap()
    build_vit(nc, *args, out)
    r = run_bass_kernel_spmd(nc, [{f"in_{k}": v for k, v in arrays.items()}], core_ids=[0])
    return r.results[0]["out_0"]
```

```python
from contextlib import ExitStack

import concourse.bass as bass
from concourse import mybir

F32 = mybir.dt.float32
F16 = mybir.dt.float16
I32 = mybir.dt.int32
ALU = mybir.AluOpType
ACT = mybir.ActivationFunctionType
AX_X = mybir.AxisListType.X

EPS = 1e-5
PATCH = 16
HALF = PATCH // 2
CH = 3
D = 192
HEADS = 12
HD = D // HEADS
HW = 32
KC = 96
NKC = D // KC
E = 3
FF = 768
FC = FF // 128

S_ACT = 32.0
S_W = 256.0
S_QK = 64.0
S_HID = 16.0

EPS_QK = HD * EPS * (S_ACT * S_W) ** 2
NEWTON = 3


class Image:

    images = 0

    def __init__(self, engine, index, position):
        self.engine, self.index, self.position, self.kept = engine, index, position, {}

    def upto(self, d):
        if isinstance(self.index, int):
            return self.index + d + 1
        if d not in self.kept:
            self.kept[d] = self.engine.snap(self.index + (d + 1))
        return self.kept[d]

    def has(self, d):
        return not isinstance(self.index, int) or self.index + d < self.images

    def slot(self, d, slots=2):
        return (self.position + d) % slots


def wait(engine, sem, count):
    if not isinstance(count, int) or count > 0:
        engine.wait_ge(sem, count)


def build_vit(nc, own, opposite, tokW, tokGamma, tokBeta, tokB, qkvW, projW, gateW, W1, b1, W2, b2, out):
    B = Image.images = own.shape[0]
    G = own.shape[3]
    CB = own.shape[2]
    SIDE = 14
    T = G // 2
    PD = CH * PATCH * PATCH
    OPP = SIDE + 1

    h1_dram = nc.dram_tensor("h1_scratch", [B, T, 2 * D], F32).ap()
    y2_dram = nc.dram_tensor("y2_scratch", [B, KC, 2 * NKC * G], F16).ap()

    with ExitStack() as ctx:
        def sem(name):
            return ctx.enter_context(nc.semaphore(name))

        WORDS = 54000
        arena = ctx.enter_context(nc.sbuf_tensor("arena", [128, WORDS], F32))
        used = [0]
        peak = [0]

        def take(parts, *dims, dt=F32):
            n = 1
            for x in dims:
                n *= x
            words = n if dt in (F32, I32) else (n + 1) // 2
            words = (words + 7) // 8 * 8
            at = used[0]
            used[0] += words
            peak[0] = max(peak[0], used[0])
            assert used[0] <= WORDS, used[0]
            v = arena[0:parts, at:at + (n if dt in (F32, I32) else n // 2)]
            if dt != F32:
                v = v.bitcast(dt)
            if len(dims) > 1:
                names = [f"d{k}" for k in range(len(dims))]
                v = v.rearrange("p (" + " ".join(names) + ") -> p " + " ".join(names), **dict(zip(names, dims)))
            return v

        ident = take(128, 128)
        ident16 = take(128, 128, dt=F16)
        ones = take(128, 128)
        eps_ln = take(T, 2)
        minus_half = take(T, 2)
        gate_w = take(KC, NKC, E)
        gate_sum = take(KC, B, NKC)
        after_shared = used[0]

        tok_w = take(128, CB, D + 1)
        tok_bias = take(T, D)
        qkv_w = take(KC, 2, NKC, 3 * D, dt=F16)
        proj_w = take(KC, 2, NKC, D, dt=F16)
        own_x = [take(128, CB * G) for _ in range(2)]
        opp_x = [take(128, CB, OPP, OPP) for _ in range(2)]
        row_sum = take(128, CB, SIDE, OPP)
        xcat = [take(128, CB, G) for _ in range(2)]
        xsq = take(128, CB, G)
        xsq_sum = take(128, G)
        tok_mean = take(T, 2)
        tok_mean2 = take(T, 2)
        tok_var = take(T, 2)
        tok_rstd = take(T, 2)
        tok_sh, sh1, sh2 = take(T, 2), take(T, 2), take(T, 2)
        qk_var = take(T, 4 * HEADS)
        qk_t = take(T, 4 * HEADS)
        h0 = [take(T, 2, D) for _ in range(4)]
        y = take(T, 2, D)
        yT = take(KC, 2, NKC * G, dt=F16)
        bn1 = take(T, 2, 6)
        mv1 = take(T, 2, 2)
        rstd1 = take(T, 2)
        qk_sq = take(T, 2, 2 * HEADS, HD + 1)
        qk_rs = take(T, 4 * HEADS)
        qk_n = take(T, 2, 2 * HEADS, HD)
        q_st = take(T, 2 * HEADS, 4 * HD, dt=F16)
        k_st = take(T, 2 * HEADS, 4 * HD, dt=F16)
        q_even = [take(128, HEADS // 2, G, dt=F16) for _ in range(2)]
        q_odd = [take(128, HEADS // 2, G, dt=F16) for _ in range(2)]
        kT = [take(128, HEADS // 2, G, dt=F16) for _ in range(2)]
        val = [take(T, 2, HEADS, HW) for _ in range(2)]
        prob = [take(T, 2 * G) for _ in range(HEADS)]
        oT = take(128, 3, G)
        rden = take(T, 2, HEADS)
        attn = take(T, 2, D)
        aT = take(KC, 2, NKC * G, dt=F16)
        h1 = [take(T, 2, D) for _ in range(2)]
        bn2 = take(T, 2, 6)
        mv2 = take(T, 2, 2)
        rstd2 = take(T, 2)
        y2 = take(T, 2, D)
        y2T = [take(KC, 2, NKC * G, dt=F16) for _ in range(2)]
        keep = used[0]
        used[0] = keep
        tok_raw = take(128, CB, D)
        tok_gam = take(128, CB)
        tok_bet = take(128, CB)
        beta_cols = take(128, CB, T)
        tok_b = take(T, D)
        qkv_raw = take(KC, NKC, 3 * D)
        qkv_gs = take(KC, NKC, 2 * HEADS)
        proj_raw = take(KC, NKC, D)

        used[0] = after_shared
        w1_raw = take(KC + 1, E, NKC, FF)
        w2_raw = take(128, E, FC, D)
        b2_all = take(T, E * D)
        w1_all = take(KC + 1, E * 2 * NKC * FF, dt=F16)
        w2_all = take(128, E * 2 * FC * D, dt=F16)
        w1_sel = [take(KC + 1, 2, NKC, FF, dt=F16) for _ in range(2)]
        w2_sel = [take(128, 2, FC, D, dt=F16) for _ in range(2)]
        x2 = [take(KC + 1, 2, NKC, G, dt=F16) for _ in range(2)]
        h1_in = [take(T, 2, D) for _ in range(2)]
        hid = [take(128, 2 * G) for _ in range(3)]
        hidT = [take(128, 2, 2 * G, dt=F16) for _ in range(3)]
        y_out = [take(T, 2, D) for _ in range(2)]
        y_fin = [take(T, 2, D) for _ in range(2)]
        g_logit = take(B, E)
        g_max = take(B, 1)
        g_sub = take(B, E)
        g_exp = take(B, E)
        g_sum = take(B, 1)
        g_pair = take(B, 2)
        g_is = take(B, E)
        g_not = take(B, 2)
        g_wide = take(B, 2, T)
        gate = take(T, B)
        expert_f = take(1, B)
        expert = take(1, B, dt=I32)

        bank = [ctx.enter_context(nc.psum_tensor(f"bank{n}", [128, 512], F32)) for n in range(8)]
        S = bank[0:2]
        O = bank[2:4]
        W = bank[4]
        X, Y, Z = bank[5:8]
        Y16, Z16 = Y[:, :].bitcast(F16), Z[:, :].bitcast(F16)

        def o_bank(image_slot, g):
            return O[(image_slot + g) % 2]

        weights_in = sem("weights_in")
        const_ready = sem("const_ready")
        setup_dve = sem("setup_dve")
        setup_mm = sem("setup_mm")
        weights_ready = sem("weights_ready")
        x_in = [sem(f"x_in{n}") for n in range(2)]
        rows_added = sem("rows_added")
        cols_added = sem("cols_added")
        xcat_ready = sem("xcat_ready")
        xsq_ready = sem("xsq_ready")
        xsq_fold = [sem(f"xsq_fold{n}") for n in range(2)]
        xsq_summed = sem("xsq_summed")
        tok_ready = sem("tok_ready")
        tok_stat = [sem(f"tok_stat{n}") for n in range(4)]
        h0_ready = sem("h0_ready")
        ln1_stat = [sem(f"ln1_stat{n}") for n in range(3)]
        y_ready = sem("y_ready")
        yT_ready = sem("yT_ready")
        yT_high = sem("yT_high")
        yT_split = sem("yT_split")
        qk_ready = [sem(f"qk_ready{j}") for j in range(2)]
        v_product = sem("v_product")
        qk_squared = [sem(f"qk_squared{j}") for j in range(2)]
        qk_summed = [sem(f"qk_summed{j}") for j in range(2)]
        qk_step = [sem(f"qk_step{n}") for n in range(3 * NEWTON + 1)]
        tok_shifted, ln1_shifted, ln2_shifted = (sem(f"{n}_shifted") for n in ("tok", "ln1", "ln2"))
        qk_normed = sem("qk_normed")
        qk_high = [sem(f"{n}_high") for n in "qk"]
        qk_split = sem("qk_split")
        v_ready = sem("v_ready")
        stack_T = [sem(f"stack_T{r}") for r in range(2)]
        q_ready = [sem(f"q_ready{r}") for r in range(2)]
        k_ready = [sem(f"k_ready{r}") for r in range(2)]
        scores_ready = [sem(f"scores_ready{h}") for h in range(HEADS)]
        prob_ready = [sem(f"prob_ready{h}") for h in range(HEADS)]
        o_ready = [sem(f"o_ready{g}") for g in range(3)]
        o_out = [sem(f"o_out{g}") for g in range(3)]
        o_tokens = sem("o_tokens")
        den_inv = sem("den_inv")
        attn_ready = sem("attn_ready")
        aT_ready = sem("aT_ready")
        aT_high = sem("aT_high")
        aT_split = sem("aT_split")
        proj_ready = sem("proj_ready")
        h1_ready = sem("h1_ready")
        ln2_stat = [sem(f"ln2_stat{n}") for n in range(3)]
        y2_ready = sem("y2_ready")
        y2T_ready = sem("y2T_ready")
        y2T_high = sem("y2T_high")
        y2T_split = sem("y2T_split")
        gate_summed = sem("gate_summed")
        h1_saved = [sem(f"h1_saved{n}") for n in range(2)]
        y2_saved = [sem(f"y2_saved{n}") for n in range(2)]

        experts_in = sem("experts_in")
        rows_set = sem("rows_set")
        experts_split = sem("experts_split")
        logits_ready = sem("logits_ready")
        gate_step = sem("gate_step")
        gate_exp = sem("gate_exp")
        gate_wide = sem("gate_wide")
        gate_ready = sem("gate_ready")
        expert_known = sem("expert_known")
        x2_in = [sem(f"x2_in{n}") for n in range(2)]
        h1_back = [sem(f"h1_back{n}") for n in range(2)]
        w1_chosen = sem("w1_chosen")
        w2_chosen = sem("w2_chosen")
        hid_ready = [sem(f"hid_ready{m}") for m in range(3)]
        hid_act = [sem(f"hid_act{m}") for m in range(3)]
        hid_high = [sem(f"hid_high{m}") for m in range(3)]
        hid_split = [sem(f"hid_split{m}") for m in range(3)]
        hid_used = [sem(f"hid_used{m}") for m in range(3)]
        y_read = sem("y_read")
        y_done = sem("y_done")
        y_saved = [sem(f"y_saved{n}") for n in range(2)]

        block = ctx.enter_context(nc.Block())

        CONSTS = 9
        assert B % 4 == 0
        TURNS = (B - 8) // 4
        TURNS_2 = (B - 4) // 2

        def over_images(engine, step):
            for n in range(4):
                step(Image(engine, n, n), True, True, n > 0, n > 1)
            with engine.Fori(0, TURNS) as turn:
                for n in range(4):
                    step(Image(engine, engine.snap(turn * 4 + (n + 4)), n), True, True, True, True)
            for n in range(B - 4, B):
                step(Image(engine, n, n), n + 2 < B, n + 1 < B, True, True)

        def over_images_2(engine, step):
            step(Image(engine, 0, 0), True)
            step(Image(engine, 1, 1), True)
            with engine.Fori(0, TURNS_2) as turn:
                step(Image(engine, engine.snap(turn * 2 + 2), 0), True)
                step(Image(engine, engine.snap(turn * 2 + 3), 1), True)
            step(Image(engine, B - 2, 0), False)
            step(Image(engine, B - 1, 1), False)

        @block.sync
        def _(sp):
            def load_x(im, d):
                s = im.slot(d)
                wait(sp, rows_added, im.upto(d - 2))
                wait(sp, xcat_ready, im.upto(d - 2))
                n = im.index + d
                n = slice(n, n + 1) if isinstance(n, int) else bass.ds(n, 1)
                sp.dma_start(opp_x[s].rearrange("p a b c -> p (a b c)"),
                             opposite[n].rearrange("o p f -> (o p) f")).then_inc(x_in[s], 16)
                sp.dma_start(own_x[s], own[n].rearrange("o p c g -> (o p) (c g)")).then_inc(x_in[s], 16)

            def save_h1(im, d):
                s = im.slot(d)
                n = im.index + d
                n = slice(n, n + 1) if isinstance(n, int) else bass.ds(n, 1)
                wait(sp, h1_ready, im.upto(d))
                sp.dma_start(h1_dram[n].rearrange("o p f -> (o p) f"),
                             h1[s].rearrange("p a b -> p (a b)")).then_inc(h1_saved[s], 16)

            def save_y2(im, d):
                s = im.slot(d)
                n = im.index + d
                n = slice(n, n + 1) if isinstance(n, int) else bass.ds(n, 1)
                wait(sp, y2T_split, im.upto(d))
                sp.dma_start(y2_dram[n].rearrange("o p f -> (o p) f"),
                             y2T[s].rearrange("p a b -> p (a b)")).then_inc(y2_saved[s], 16)

            zero = Image(sp, 0, 0)
            load_x(zero, 0)
            load_x(zero, 1)
            sp.dma_start(tok_raw, tokW).then_inc(weights_in, 16)
            sp.dma_start(tok_gam, tokGamma).then_inc(weights_in, 16)
            sp.dma_start(tok_bet, tokBeta).then_inc(weights_in, 16)
            sp.dma_start(tok_b, tokB.partition_broadcast(T)).then_inc(weights_in, 16)
            sp.dma_start(qkv_raw, qkvW).then_inc(weights_in, 16)
            sp.dma_start(proj_raw, projW).then_inc(weights_in, 16)
            sp.dma_start(gate_w, gateW).then_inc(weights_in, 16)
            load_x(zero, 2)
            load_x(zero, 3)

            def step(im, patches, prepare, project, finish):
                if im.has(4):
                    load_x(im, 4)
                if finish:
                    save_y2(im, -2)
                if project:
                    save_h1(im, -1)

            over_images(sp, step)
            last = Image(sp, B, 0)
            save_y2(last, -2)
            save_h1(last, -1)
            save_y2(last, -1)
            for s in range(2):
                sp.wait_ge(h1_saved[s], 16 * (B // 2))
                sp.wait_ge(y2_saved[s], 16 * (B // 2))
            sp.wait_ge(gate_summed, B)
            sp.wait_ge(o_ready[2], B)
            for e in range(E):
                sp.dma_start(w1_raw[0:KC, e], W1[e].rearrange("(k p) f -> p k f", k=NKC)).then_inc(experts_in, 16)
                sp.dma_start(w2_raw[:, e], W2[e].rearrange("(c p) d -> p c d", c=FC)).then_inc(experts_in, 16)
            sp.dma_start(w1_raw[KC:KC + 1, :, NKC - 1, :], b1.rearrange("(o e) f -> o e f", o=1)).then_inc(experts_in, 16)
            sp.dma_start(b2_all, b2.rearrange("e d -> (e d)").partition_broadcast(T)).then_inc(experts_in, 16)

            def load_normed(im, d):
                s = im.slot(d)
                n = im.index + d
                n = slice(n, n + 1) if isinstance(n, int) else bass.ds(n, 1)
                wait(sp, hid_ready[2], im.upto(d - 2))
                sp.dma_start(x2[s][0:KC].rearrange("p a k g -> p (a k g)"),
                             y2_dram[n].rearrange("o p f -> (o p) f")).then_inc(x2_in[s], 16)

            def load_h1(im, d):
                s = im.slot(d)
                n = im.index + d
                n = slice(n, n + 1) if isinstance(n, int) else bass.ds(n, 1)
                wait(sp, y_done, im.upto(d - 2))
                sp.dma_start(h1_in[s].rearrange("p a b -> p (a b)"),
                             h1_dram[n].rearrange("o p f -> (o p) f")).then_inc(h1_back[s], 16)

            zero = Image(sp, 0, 0)
            for d in range(2):
                load_normed(zero, d)
                load_h1(zero, d)

            def step_2(im, more):
                s = im.slot(0)
                if more:
                    load_normed(im, 2)
                wait(sp, y_done, im.upto(0))
                n = im.index
                n = slice(n, n + 1) if isinstance(n, int) else bass.ds(n, 1)
                sp.dma_start(out[n].rearrange("o (j p) d -> p (o j) d", j=2), y_fin[s]).then_inc(y_saved[s], 16)
                if more:
                    load_h1(im, 2)

            over_images_2(sp, step_2)
            for s in range(2):
                sp.wait_ge(y_saved[s], 16 * (B // 2))

        @block.gpsimd
        def _(pool):
            pool.memset(ones, 1.0)
            pool.memset(eps_ln, EPS)
            pool.memset(minus_half, -0.5)
            pool.memset(qk_sq, EPS_QK)
            pool.memset(ident, 0.0).then_inc(const_ready, 1)
            pool.memset(ident16, 0.0).then_inc(const_ready, 1)
            pool.wait_ge(const_ready, 2)
            for m in (ident, ident16):
                pool.affine_select(out=m, in_=m, compare_op=ALU.not_equal, fill=1.0, base=0,
                                   pattern=[[-1, 128]], channel_multiplier=1).then_inc(const_ready, 1)
            pool.memset(q_st, 0.0)
            pool.memset(k_st, 0.0)
            for s in range(2):
                pool.memset(val[s], 0.0).then_inc(const_ready, 1)
                pool.memset(q_even[s], 0.0)
                pool.memset(q_odd[s], 0.0)
            pool.wait_ge(const_ready, 6)
            for s in range(2):
                pool.memset(val[s][:, :, :, HD:HD + 1], 1.0).then_inc(const_ready, 1)
            pool.memset(tok_w[:, :, D:D + 1], 1.0).then_inc(const_ready, 1)

            def add_rows(im, d):
                s = im.slot(d)
                n = im.index + d
                if isinstance(n, int):
                    wait(pool, x_in[s], 32 * (n // 2 + 1))
                else:
                    pool.wait_ge(x_in[s], pool.snap((n - s) * 16 + 32))
                wait(pool, cols_added, im.upto(d - 1))
                pool.tensor_tensor(row_sum, opp_x[s][:, :, 0:SIDE, :], opp_x[s][:, :, 1:OPP, :],
                                   ALU.add).then_inc(rows_added, 1)

            def add_cols(im, d):
                s = im.slot(d)
                wait(pool, rows_added, im.upto(d))
                wait(pool, tok_ready, im.upto(d - 2))
                wait(pool, xsq_ready, im.upto(d - 2))
                rows = row_sum.rearrange("p c r q -> p (c r) q")
                pool.tensor_tensor(xcat[s].rearrange("p c (r q) -> p (c r) q", q=SIDE),
                                   rows[:, :, 0:SIDE], rows[:, :, 1:OPP], ALU.add).then_inc(cols_added, 1)

            def inverse_root(dst, shifted, src, eps, ready, step, done, im, d):
                wait(pool, ready, im.upto(d))
                pool.tensor_tensor(shifted, src, eps, ALU.add).then_inc(step, 1)
                wait(pool, step, im.upto(d))
                pool.tensor_tensor(dst, shifted, minus_half, ALU.pow).then_inc(done, 1)

            def root_tokens(im, d):
                inverse_root(tok_rstd, tok_sh, tok_var, eps_ln, tok_stat[2], tok_shifted, tok_stat[3], im, d)

            def root_normed_tokens(im, d):
                inverse_root(rstd1, sh1, mv1[:, :, 1], eps_ln, ln1_stat[1], ln1_shifted, ln1_stat[2], im, d)

            def root_h1(im):
                inverse_root(rstd2, sh2, mv2[:, :, 1], eps_ln, ln2_stat[1], ln2_shifted, ln2_stat[2], im, -1)

            def sum_squares(im, d):
                wait(pool, tok_ready, im.upto(d - 1))
                wait(pool, xsq_ready, im.upto(d))
                pool.tensor_tensor(xsq[:, 0:3], xsq[:, 0:3], xsq[:, 3:6], ALU.add).then_inc(xsq_fold[0], 1)
                wait(pool, xsq_fold[0], im.upto(d))
                pool.tensor_tensor(xsq[:, 0], xsq[:, 0], xsq[:, 1], ALU.add).then_inc(xsq_fold[1], 1)
                wait(pool, xsq_fold[1], im.upto(d))
                pool.tensor_tensor(xsq_sum, xsq[:, 0], xsq[:, 2], ALU.add).then_inc(xsq_summed, 1)

            zero = Image(pool, 0, 0)
            for d in range(2):
                add_rows(zero, d)
                add_cols(zero, d)
            for d in range(2):
                sum_squares(zero, d)
                root_tokens(zero, d)
                add_rows(zero, d + 2)
                root_normed_tokens(zero, d)
                add_cols(zero, d + 2)
            sum_squares(zero, 2)

            def step(im, patches, prepare, project, finish):
                if patches:
                    root_tokens(im, 2)
                    root_normed_tokens(im, 2)
                if im.has(4):
                    add_rows(im, 4)
                if project:
                    root_h1(im)
                if im.has(4):
                    add_cols(im, 4)
                if im.has(3):
                    sum_squares(im, 3)

            over_images(pool, step)
            root_h1(Image(pool, B, 0))

        @block.scalar
        def _(act):
            def square_x(im, d):
                s = im.slot(d)
                wait(act, xcat_ready, im.upto(d))
                wait(act, xsq_summed, im.upto(d - 1))
                act.activation(xsq, xcat[s], ACT.Square).then_inc(xsq_ready, 1)

            def high(psum, dst, ready, prev_used, done, im, d):
                wait(act, ready, im.upto(d))
                for sem_, n in prev_used:
                    wait(act, sem_, n)
                act.activation(dst[:, 0], psum[0:KC, 0:NKC * G], ACT.Copy, scale=S_ACT).then_inc(done, 1)

            def high_y(im, d):
                high(X, yT, yT_ready, [(v_product, im.upto(d - 1))], yT_high, im, d)

            def square_qk(im, d, j):
                wait(act, qk_ready[j], im.upto(d))
                wait(act, qk_summed[j], im.upto(d - 1))
                act.activation(qk_sq[:, j, :, 0:HD], (Y, Z)[j][0:T, 0:2 * D].rearrange("p (h e) -> p h e", e=HD),
                               ACT.Square).then_inc(qk_squared[j], 1)

            def high_qk(im, d):
                wait(act, qk_normed, im.upto(d))
                wait(act, stack_T[1], im.upto(d - 1))
                for n, (dst, blocks) in enumerate(((q_st, slice(0, 3, 2)), (k_st, slice(0, 2)))):
                    act.activation(
                        dst.rearrange("p h (b e) -> p h b e", b=4)[:, :, blocks, :],
                        qk_n[:, n].unsqueeze(2).to_broadcast([T, 2 * HEADS, 2, HD]), ACT.Copy,
                        scale=S_QK).then_inc(qk_high[n], 1)

            def values(im, d):
                s = im.slot(d)
                wait(act, v_product, im.upto(d))
                wait(act, o_ready[2], im.upto(d - 2))
                act.activation(val[s][:, :, :, 0:HD].rearrange("p k h e -> p (k h) e"),
                               X[0:T, 0:2 * D].rearrange("p (h e) -> p h e", e=HD),
                               ACT.Copy, scale=1.0 / (S_ACT * S_W)).then_inc(v_ready, 1)

            def keys(im, d, r):
                s = im.slot(d)
                wait(act, stack_T[r], im.upto(d))
                wait(act, scores_ready[HEADS - 1], im.upto(d - 2))
                act.copy(kT[s][:, 3 * r:3 * r + 3, :].rearrange("p h g -> p (h g)"),
                         Y16[:, 0:3 * G]).then_inc(k_ready[r], 1)

            def exps(im, d, h):
                wait(act, scores_ready[h], im.upto(d))
                wait(act, o_ready[h // 4], im.upto(d - 1))
                act.activation(prob[h], S[h % 2][0:T, 0:2 * G], ACT.Exp,
                               scale=HD ** 0.5 / (S_QK * S_QK)).then_inc(prob_ready[h], 1)

            def o_copy(im, d, g):
                wait(act, o_ready[g], im.upto(d))
                wait(act, o_tokens, im.upto(d - 1))
                act.copy(oT[:, g, :], o_bank(im.slot(d), g)[:, 0:G]).then_inc(o_out[g], 1)

            def high_a(im):
                high(W, aT, aT_ready, [(proj_ready, im.upto(-2))], aT_high, im, -1)

            def high_y2(im, d):
                n = im.index + d
                s = im.slot(d)
                if isinstance(n, int):
                    prev = [(y2_saved[s], 16 * (n // 2))]
                else:
                    prev = [(y2_saved[s], act.snap((n - s) * 8))]
                high(W, y2T[s], y2T_ready, prev, y2T_high, im, d)

            act.wait_ge(weights_ready, 1)
            zero = Image(act, 0, 0)
            square_x(zero, 0)
            square_x(zero, 1)
            high_y(zero, 0)
            square_qk(zero, 0, 0)
            square_qk(zero, 0, 1)
            values(zero, 0)
            high_qk(zero, 0)
            square_x(zero, 2)
            keys(zero, 0, 0)
            keys(zero, 0, 1)
            exps(zero, 0, 0)
            exps(zero, 0, 1)
            high_y(zero, 1)
            exps(zero, 0, 2)

            def step(im, patches, prepare, project, finish):
                exps(im, 0, 3)
                exps(im, 0, 4)
                if prepare:
                    square_qk(im, 1, 0)
                    square_qk(im, 1, 1)
                    values(im, 1)
                exps(im, 0, 5)
                if finish:
                    high_y2(im, -2)
                exps(im, 0, 6)
                if prepare:
                    high_qk(im, 1)
                exps(im, 0, 7)
                if project:
                    high_a(im)
                o_copy(im, 0, 0)
                exps(im, 0, 8)
                o_copy(im, 0, 1)
                exps(im, 0, 9)
                if prepare:
                    keys(im, 1, 0)
                exps(im, 0, 10)
                if im.has(3):
                    square_x(im, 3)
                exps(im, 0, 11)
                if prepare:
                    keys(im, 1, 1)
                    exps(im, 1, 0)
                o_copy(im, 0, 2)
                if prepare:
                    exps(im, 1, 1)
                if patches:
                    high_y(im, 2)
                if prepare:
                    exps(im, 1, 2)

            over_images(act, step)
            last = Image(act, B, 0)
            high_y2(last, -2)
            high_a(last)
            high_y2(last, -1)

            act.wait_ge(gate_step, 3)
            act.activation(g_exp, g_sub, ACT.Exp).then_inc(gate_exp, 1)

            def hidden(im, d):
                for m in range(3):
                    wait(act, hid_ready[m], im.upto(d))
                    wait(act, hid_split[m], im.upto(d - 1))
                    act.activation(hid[m], bank[m][:, 0:2 * G], ACT.Gelu,
                                   scale=1.0 / (S_ACT * S_W)).then_inc(hid_act[m], 1)
                    wait(act, hid_act[m], im.upto(d))
                    wait(act, hid_used[m], im.upto(d - 1))
                    act.activation(hidT[m][:, 0], hid[m], ACT.Copy, scale=S_HID).then_inc(hid_high[m], 1)

            hidden(Image(act, 0, 0), 0)

            def step_2(im, more):
                if more or im.index + 1 < B:
                    hidden(im, 1)

            over_images_2(act, step_2)

        @block.vector
        def _(dve):
            done = [0]

            def self_step(ins):
                done[0] += 1
                ins.then_inc(setup_dve, 1)
                dve.wait_ge(setup_dve, done[0])

            dve.wait_ge(weights_in, 16 * 7)
            dve.wait_ge(const_ready, CONSTS)
            self_step(dve.tensor_tensor(tok_w[:, :, 0:D], tok_raw,
                                        tok_gam.unsqueeze(2).to_broadcast([128, CB, D]), ALU.mult))
            self_step(dve.tensor_copy(beta_cols, tok_bet.unsqueeze(2).to_broadcast([128, CB, T])))
            self_step(dve.tensor_reduce(qkv_gs, qkv_raw[:, :, 0:2 * D].rearrange("p k (g e) -> p k g e", e=HD),
                                        AX_X, ALU.add))
            for k in range(NKC):
                self_step(dve.scalar_tensor_tensor(
                    qkv_raw[:, k, 0:2 * D].rearrange("p (g e) -> p g e", e=HD),
                    qkv_gs[:, k].unsqueeze(2).to_broadcast([KC, 2 * HEADS, HD]), -1.0 / HD,
                    qkv_raw[:, k, 0:2 * D].rearrange("p (g e) -> p g e", e=HD), ALU.mult, ALU.add))
            self_step(dve.tensor_scalar(qkv_w[:, 0], qkv_raw, S_W, None, ALU.mult))
            self_step(dve.scalar_tensor_tensor(qkv_w[:, 1], qkv_raw, S_W, qkv_w[:, 0], ALU.mult, ALU.subtract))
            self_step(dve.tensor_scalar(proj_w[:, 0], proj_raw, S_W, None, ALU.mult))
            self_step(dve.scalar_tensor_tensor(proj_w[:, 1], proj_raw, S_W, proj_w[:, 0], ALU.mult, ALU.subtract))
            dve.wait_ge(setup_mm, 1)
            self_step(dve.scalar_tensor_tensor(
                tok_w[:, :, 0:D], X[:, 0:D].unsqueeze(1).to_broadcast([128, CB, D]), -1.0 / PD,
                tok_w[:, :, 0:D], ALU.mult, ALU.add))
            dve.tensor_tensor(tok_bias, Y[0:T, 0:D], tok_b, ALU.add).then_inc(weights_ready, 1)

            def add_own(im, d, c=None):
                s = im.slot(d)
                if not c:
                    wait(dve, cols_added, im.upto(d))
                cols = slice(0, CB * G) if c is None else slice(c * G, (c + 1) * G)
                flat = xcat[s].rearrange("p c g -> p (c g)")[:, cols]
                last = dve.tensor_tensor(flat, flat, own_x[s][:, cols], ALU.add)
                if c is None or c == CB - 1:
                    last.then_inc(xcat_ready, 1)

            def norm_stats(src, src_ready, bn, mv, steps, im, d):
                wait(dve, src_ready, im.upto(d))
                for j in range(2):
                    last = dve.bn_stats(bn[:, j], src[:, j])
                last.then_inc(steps[0], 1)
                dve.wait_ge(weights_ready, 1)
                wait(dve, steps[0], im.upto(d))
                for j in range(2):
                    last = dve.bn_aggr(mv[:, j], bn[:, j])
                last.then_inc(steps[1], 1)

            def norm_apply(src, dst, mv, rstd, steps, dst_ready, im, d):
                wait(dve, steps[2], im.upto(d))
                for j in range(2):
                    last = dve.tensor_scalar(dst[:, j], src[:, j], mv[:, j, 0:1], rstd[:, j:j + 1],
                                             ALU.subtract, ALU.mult)
                last.then_inc(dst_ready, 1)

            def token_stats(im, d):
                wait(dve, tok_ready, im.upto(d))
                sums = X[0:T, D:2 * (D + 1):D + 1]
                dve.tensor_scalar(tok_mean, sums, 1.0 / PD, None, ALU.mult).then_inc(tok_stat[0], 1)
                wait(dve, tok_stat[0], im.upto(d))
                dve.scalar_tensor_tensor(tok_mean2, sums, 1.0 / PD, tok_mean, ALU.mult, ALU.mult).then_inc(tok_stat[1], 1)
                wait(dve, tok_stat[1], im.upto(d))
                dve.scalar_tensor_tensor(tok_var, X[0:T, 2 * (D + 1):2 * (D + 1) + 2], 1.0 / PD, tok_mean2,
                                         ALU.mult, ALU.subtract).then_inc(tok_stat[2], 1)

            def tokens(im, d):
                wait(dve, tok_stat[3], im.upto(d))
                wait(dve, h1_ready, im.upto(d - 4))
                for j in range(2):
                    last = dve.scalar_tensor_tensor(h0[im.slot(d, 4)][:, j], X[0:T, j * (D + 1):j * (D + 1) + D],
                                                    tok_rstd[:, j:j + 1], tok_bias, ALU.mult, ALU.add)
                last.then_inc(h0_ready, 1)

            def stats_tokens(im, d):
                norm_stats(h0[im.slot(d, 4)], h0_ready, bn1, mv1, ln1_stat, im, d)

            def norm_tokens(im, d):
                wait(dve, yT_ready, im.upto(d - 1))
                norm_apply(h0[im.slot(d, 4)], y, mv1, rstd1, ln1_stat, y_ready, im, d)

            def low(psum, dst, high_done, split, im, d):
                wait(dve, high_done, im.upto(d))
                dve.scalar_tensor_tensor(dst[:, 1], psum[0:KC, 0:NKC * G], S_ACT, dst[:, 0],
                                         ALU.mult, ALU.subtract).then_inc(split, 1)

            def sum_qk(im, d, j):
                wait(dve, qk_squared[j], im.upto(d))
                dve.tensor_reduce(qk_var[:, j * 2 * HEADS:(j + 1) * 2 * HEADS], qk_sq[:, j], AX_X,
                                  ALU.add).then_inc(qk_summed[j], 1)

            def norm_qk(im, d, ahead=False):
                wait(dve, qk_summed[0], im.upto(d))
                wait(dve, qk_summed[1], im.upto(d))
                dve.tensor_scalar(qk_rs.bitcast(I32), qk_var.bitcast(I32), -0.5, float(0x5F3759DF),
                                  ALU.mult, ALU.add).then_inc(qk_step[0], 1)
                for n in range(NEWTON):
                    if ahead:
                        add_own(im, 3, 2 * n)
                    wait(dve, qk_step[3 * n + 0], im.upto(d))
                    dve.scalar_tensor_tensor(qk_t, qk_rs, -0.5, qk_rs, ALU.mult, ALU.mult).then_inc(qk_step[3 * n + 1], 1)
                    wait(dve, qk_step[3 * n + 1], im.upto(d))
                    dve.tensor_tensor(qk_t, qk_t, qk_var, ALU.mult).then_inc(qk_step[3 * n + 2], 1)
                    if ahead:
                        add_own(im, 3, 2 * n + 1)
                    wait(dve, qk_step[3 * n + 2], im.upto(d))
                    dve.scalar_tensor_tensor(qk_rs, qk_t, 1.5, qk_rs, ALU.add, ALU.mult).then_inc(qk_step[3 * n + 3], 1)
                wait(dve, qk_step[3 * NEWTON], im.upto(d))
                wait(dve, qk_high[1], im.upto(d - 1))
                for j in range(2):
                    rs = qk_rs[:, j * 2 * HEADS:(j + 1) * 2 * HEADS].rearrange("p (a h) -> p a h", a=2)
                    last = dve.tensor_tensor(
                        qk_n[:, :, j * HEADS:(j + 1) * HEADS, :],
                        (Y, Z)[j][0:T, 0:2 * D].rearrange("p (a h e) -> p a h e", a=2, e=HD),
                        rs.unsqueeze(3).to_broadcast([T, 2, HEADS, HD]), ALU.mult)
                last.then_inc(qk_normed, 1)

            def low_qk(im, d):
                wait(dve, qk_high[0], im.upto(d))
                dve.scalar_tensor_tensor(q_st[:, :, HD:2 * HD], qk_n[:, 0], S_QK, q_st[:, :, 0:HD],
                                         ALU.mult, ALU.subtract)
                wait(dve, qk_high[1], im.upto(d))
                dve.scalar_tensor_tensor(k_st[:, :, 2 * HD:3 * HD], qk_n[:, 1], S_QK, k_st[:, :, 0:HD],
                                         ALU.mult, ALU.subtract).then_inc(qk_split, 1)

            def queries(im, d, r):
                s = im.slot(d)
                wait(dve, stack_T[r], im.upto(d))
                wait(dve, scores_ready[HEADS - 1], im.upto(d - 2))
                for dst, lo in ((q_even[s], 0), (q_odd[s], 64)):
                    last = dve.tensor_copy(dst[lo:lo + 64, 3 * r:3 * r + 3, :].rearrange("p h g -> p (h g)"),
                                           Z16[lo:lo + 64, 0:3 * G])
                last.then_inc(q_ready[r], 1)

            def norm_attn(im, d):
                wait(dve, o_tokens, im.upto(d))
                wait(dve, aT_ready, im.upto(d - 1))
                src = [t[0:T, 0:3 * 128].rearrange("p (h w) -> p h w", w=HW)
                       for t in (W, o_bank(im.slot(d), 2))]
                for j in range(2):
                    last = dve.reciprocal(rden[:, j], src[j][:, :, HD])
                last.then_inc(den_inv, 1)
                wait(dve, den_inv, im.upto(d))
                for j in range(2):
                    last = dve.tensor_tensor(attn[:, j].rearrange("p (h e) -> p h e", e=HD), src[j][:, :, 0:HD],
                                             rden[:, j].unsqueeze(2).to_broadcast([T, HEADS, HD]), ALU.mult)
                last.then_inc(attn_ready, 1)

            def residual(im):
                s = im.slot(-1)
                n = im.index - 1
                if isinstance(n, int):
                    wait(dve, h1_saved[s], 16 * (n // 2))
                else:
                    dve.wait_ge(h1_saved[s], dve.snap((n - s) * 8))
                wait(dve, proj_ready, im.upto(-1))
                dve.scalar_tensor_tensor(h1[s].rearrange("p a b -> p (a b)"), W[0:T, 0:2 * D], 1.0 / (S_ACT * S_W),
                                         h0[im.slot(-1, 4)].rearrange("p a b -> p (a b)"),
                                         ALU.mult, ALU.add).then_inc(h1_ready, 1)

            def stats_h1(im):
                norm_stats(h1[im.slot(-1)], h1_ready, bn2, mv2, ln2_stat, im, -1)

            def norm_h1(im):
                wait(dve, y2T_ready, im.upto(-2))
                norm_apply(h1[im.slot(-1)], y2, mv2, rstd2, ln2_stat, y2_ready, im, -1)

            def low_y2(im, d):
                low(W, y2T[im.slot(d)], y2T_high, y2T_split, im, d)

            def gate_sums(im, d):
                n = im.index + d
                at = n if isinstance(n, int) else dve.snap(n)
                dst = gate_sum[:, at, :] if isinstance(n, int) else gate_sum[:, bass.ds(at, 1), :].rearrange("p o k -> p (o k)")
                dve.tensor_reduce(dst, W[0:KC, 0:NKC * G].rearrange("p (k g) -> p k g", g=G), AX_X,
                                  ALU.add).then_inc(gate_summed, 1)

            zero = Image(dve, 0, 0)
            add_own(zero, 0)
            dve.wait_ge(weights_ready, 1)
            add_own(zero, 1)
            token_stats(zero, 0)
            tokens(zero, 0)
            stats_tokens(zero, 0)
            norm_tokens(zero, 0)
            low(X, yT, yT_high, yT_split, zero, 0)
            sum_qk(zero, 0, 0)
            sum_qk(zero, 0, 1)
            norm_qk(zero, 0)
            low_qk(zero, 0)
            add_own(zero, 2)
            queries(zero, 0, 0)
            queries(zero, 0, 1)
            token_stats(zero, 1)
            tokens(zero, 1)
            stats_tokens(zero, 1)
            norm_tokens(zero, 1)
            low(X, yT, yT_high, yT_split, zero, 1)

            def step(im, patches, prepare, project, finish):
                if prepare:
                    sum_qk(im, 1, 0)
                    sum_qk(im, 1, 1)
                    norm_qk(im, 1, im.has(3))
                if finish:
                    low_y2(im, -2)
                    gate_sums(im, -2)
                if patches:
                    token_stats(im, 2)
                if prepare:
                    low_qk(im, 1)
                if patches:
                    tokens(im, 2)
                if project:
                    low(W, aT, aT_high, aT_split, im, -1)
                if patches:
                    stats_tokens(im, 2)
                if prepare:
                    queries(im, 1, 0)
                if patches:
                    norm_tokens(im, 2)
                if project:
                    residual(im)
                    stats_h1(im)
                if patches:
                    low(X, yT, yT_high, yT_split, im, 2)
                if prepare:
                    queries(im, 1, 1)
                if project:
                    norm_h1(im)
                norm_attn(im, 0)

            over_images(dve, step)
            last = Image(dve, B, 0)
            low_y2(last, -2)
            gate_sums(last, -2)
            low(W, aT, aT_high, aT_split, last, -1)
            residual(last)
            stats_h1(last)
            norm_h1(last)
            low_y2(last, -1)
            gate_sums(last, -1)

            dve.wait_ge(h1_saved[1], 16 * (B // 2))
            dve.wait_ge(o_ready[2], B)
            dve.wait_ge(aT_ready, B)
            dve.wait_ge(gate_summed, B)
            dve.memset(w1_raw[KC:KC + 1, :, 0, :], 0.0)
            for s in range(2):
                dve.memset(x2[s][KC:KC + 1], 0.0).then_inc(rows_set, 1)
            dve.wait_ge(rows_set, 2)
            for s in range(2):
                dve.memset(x2[s][KC:KC + 1, 0, NKC - 1], S_ACT).then_inc(rows_set, 1)
            gates = [0]

            def gate_do(ins):
                gates[0] += 1
                ins.then_inc(gate_step, 1)
                dve.wait_ge(gate_step, gates[0])

            dve.wait_ge(logits_ready, 1)
            gate_do(dve.tensor_scalar(g_logit, X[0:B, 0:E], 1.0 / G, None, ALU.mult))
            gate_do(dve.tensor_reduce(g_max, g_logit, AX_X, ALU.max))
            gate_do(dve.tensor_scalar(g_sub, g_logit, g_max[:, 0:1], None, ALU.subtract))
            gate_do(dve.tensor_scalar(g_is, g_sub, 0.0, None, ALU.is_ge))
            for n in range(2):
                gate_do(dve.tensor_scalar(g_not[:, n:n + 1], g_is[:, n:n + 1], -1.0, float(n + 1), ALU.mult, ALU.add))
            gate_do(dve.tensor_tensor(g_pair[:, 1:2], g_not[:, 0:1], g_not[:, 1:2], ALU.mult))
            dve.wait_ge(gate_exp, 1)
            gate_do(dve.tensor_reduce(g_sum, g_exp, AX_X, ALU.add))
            gate_do(dve.reciprocal(g_pair[:, 0:1], g_sum))
            dve.tensor_copy(g_wide, g_pair.unsqueeze(2).to_broadcast([B, 2, T])).then_inc(gate_wide, 1)
            dve.wait_ge(gate_ready, 1)
            gate_do(dve.tensor_copy(gate, Y[0:T, 0:B]))
            gate_do(dve.tensor_copy(expert_f, Y[0:1, B:2 * B]))
            dve.tensor_copy(expert, expert_f).then_inc(expert_known, 1)
            dve.wait_ge(expert_known, 1)

            dve.wait_ge(experts_in, 16 * (2 * E + 2))
            w1_v = w1_all.rearrange("p (e a n) -> p e a n", e=E, a=2)
            w2_v = w2_all.rearrange("p (e a n) -> p e a n", e=E, a=2)
            for v, raw in ((w1_v, w1_raw.rearrange("p e k f -> p e (k f)")), (w2_v, w2_raw.rearrange("p e c d -> p e (c d)"))):
                gate_do(dve.tensor_scalar(v[:, :, 0], raw, S_W, None, ALU.mult))
                gate_do(dve.scalar_tensor_tensor(v[:, :, 1], raw, S_W, v[:, :, 0], ALU.mult, ALU.subtract))

            N1, N2 = 2 * NKC * FF, 2 * FC * D

            def expert_of(im, d):
                n = im.index + d
                at = expert[0:1, n:n + 1] if isinstance(n, int) else expert[0:1, bass.ds(n, 1)]
                return dve.value_load(at, min_val=0, max_val=E - 1)

            def choose_w1(im, d, e):
                s = im.slot(d)
                wait(dve, hid_ready[2], im.upto(d - 2))
                dve.tensor_copy(w1_sel[s].rearrange("p a k f -> p (a k f)"),
                                w1_all[:, bass.ds(dve.snap(e * N1), N1)]).then_inc(w1_chosen, 1)

            def choose_w2(im, d, e):
                s = im.slot(d)
                wait(dve, hid_used[2], im.upto(d - 2))
                dve.tensor_copy(w2_sel[s].rearrange("p a c d -> p (a c d)"),
                                w2_all[:, bass.ds(dve.snap(e * N2), N2)]).then_inc(w2_chosen, 1)

            def low_hidden(im, d):
                for m in range(3):
                    wait(dve, hid_high[m], im.upto(d))
                    dve.scalar_tensor_tensor(hidT[m][:, 1], hid[m], S_HID, hidT[m][:, 0],
                                             ALU.mult, ALU.subtract).then_inc(hid_split[m], 1)

            def finish(im, e):
                s = im.slot(0)
                n = im.index
                bias = b2_all[:, bass.ds(dve.snap(e * D), D)]
                wait(dve, hid_used[2], im.upto(0))
                for j in range(2):
                    last = dve.scalar_tensor_tensor(y_out[s][:, j], bank[3 + 2 * s + j][0:T, 0:D], 1.0 / (S_HID * S_W),
                                                    bias, ALU.mult, ALU.add)
                last.then_inc(y_read, 1)
                if isinstance(n, int):
                    wait(dve, h1_back[s], 16 * (n // 2 + 1))
                    wait(dve, y_saved[s], 16 * (n // 2))
                else:
                    dve.wait_ge(h1_back[s], dve.snap((n - s) * 8 + 16))
                    dve.wait_ge(y_saved[s], dve.snap((n - s) * 8))
                wait(dve, y_read, im.upto(0))
                g = gate[:, n:n + 1] if isinstance(n, int) else gate[:, bass.ds(n, 1)]
                dve.scalar_tensor_tensor(y_fin[s], y_out[s], g, h1_in[s], ALU.mult, ALU.add).then_inc(y_done, 1)

            zero = Image(dve, 0, 0)
            for d in range(2):
                e = expert_of(zero, d)
                choose_w1(zero, d, e)
                choose_w2(zero, d, e)
            low_hidden(zero, 0)

            def step_2(im, more):
                if more:
                    ahead = expert_of(im, 2)
                    choose_w1(im, 2, ahead)
                if more or im.index + 1 < B:
                    low_hidden(im, 1)
                finish(im, expert_of(im, 0))
                if more:
                    choose_w2(im, 2, ahead)

            over_images_2(dve, step_2)

        @block.tensor
        def _(pe):
            def split_product(dst, left, right, cols, groups, start_first=True):
                pairs = [(a, b, k) for a, b in ((0, 0), (0, 1), (1, 0)) for k in range(groups)]
                for n, (a, b, k) in enumerate(pairs):
                    last = pe.matmul(dst, left(a, k), right(b, k)[:, cols], start=(n == 0), stop=(n == len(pairs) - 1))
                return last

            pe.wait_ge(const_ready, CONSTS)
            pe.wait_ge(setup_dve, 2)
            for c in range(CB):
                pe.matmul(X[:, 0:D], ones[:, :], tok_w[:, c, 0:D], start=(c == 0), stop=(c == CB - 1))
            for c in range(CB):
                last = pe.matmul(Y[0:T, 0:D], beta_cols[:, c], tok_raw[:, c], start=(c == 0), stop=(c == CB - 1))
            last.then_inc(setup_mm, 1)

            def patches_mm(im, d, j):
                s = im.slot(d)
                if j == 0:
                    wait(pe, xcat_ready, im.upto(d))
                    wait(pe, v_ready, im.upto(d - 1))
                for c in range(CB):
                    pe.matmul(X[0:T, j * (D + 1):(j + 1) * (D + 1)], xcat[s][:, c, j * T:(j + 1) * T], tok_w[:, c],
                              start=(c == 0), stop=(c == CB - 1))
                if j == 1:
                    wait(pe, xsq_summed, im.upto(d))
                    for jj in range(2):
                        last = pe.matmul(X[0:T, 2 * (D + 1) + jj:2 * (D + 1) + jj + 1],
                                         xsq_sum[:, jj * T:(jj + 1) * T], ones[:, 0:1], start=True, stop=True)
                    last.then_inc(tok_ready, 1)

            def turn(dst, src, done):
                for k in range(NKC):
                    for j in range(2):
                        last = pe.transpose(dst[0:KC, k * G + j * T:k * G + (j + 1) * T],
                                            src[:, j, k * KC:(k + 1) * KC], ident[0:T, 0:T])
                last.then_inc(done, 1)

            def turn_y(im, d):
                wait(pe, y_ready, im.upto(d))
                turn(X, y, yT_ready)

            def queries_keys_mm(im, d, j):
                if j == 0:
                    wait(pe, yT_split, im.upto(d))
                wait(pe, (k_ready, q_ready)[j][1], im.upto(d - 1))
                left = lambda a, k: yT[:, a, k * G + j * T:k * G + (j + 1) * T]
                right = lambda b, k: qkv_w[:, b, k]
                split_product((Y, Z)[j][0:T, 0:2 * D], left, right, slice(0, 2 * D), NKC).then_inc(qk_ready[j], 1)

            def values_mm(im, d):
                wait(pe, yT_split, im.upto(d))
                for j in range(2):
                    last = split_product(X[0:T, j * D:(j + 1) * D],
                                         lambda a, k: yT[:, a, k * G + j * T:k * G + (j + 1) * T],
                                         lambda b, k: qkv_w[:, b, k], slice(2 * D, 3 * D), NKC)
                last.then_inc(v_product, 1)

            def turn_qk(im, d, r):
                if r == 0:
                    wait(pe, qk_split, im.upto(d))
                else:
                    wait(pe, q_ready[0], im.upto(d))
                    wait(pe, k_ready[0], im.upto(d))
                for p in range(3):
                    for j in range(2):
                        h = j * HEADS + 2 * (3 * r + p)
                        at = slice(p * G + j * T, p * G + (j + 1) * T)
                        for dst, st in ((Z16, q_st), (Y16, k_st)):
                            last = pe.transpose(dst[:, at], st[:, h:h + 2, :].rearrange("p h e -> p (h e)"),
                                                ident16[0:T, 0:T])
                last.then_inc(stack_T[r], 1)

            def scores(im, d, h):
                s = im.slot(d)
                if h % 6 == 0:
                    wait(pe, q_ready[h // 6], im.upto(d))
                    wait(pe, k_ready[h // 6], im.upto(d))
                wait(pe, prob_ready[(h - 2) % HEADS], im.upto(d if h >= 2 else d - 1))
                q = (q_even, q_odd)[h % 2][s]
                for k in range(2):
                    last = pe.matmul(S[h % 2][0:T, k * G:(k + 1) * G], kT[s][:, h // 2, k * T:(k + 1) * T],
                                     q[:, h // 2, :], start=True, stop=True)
                last.then_inc(scores_ready[h], 1)

            def weigh(im, d, g):
                s = im.slot(d)
                wait(pe, prob_ready[4 * g + 3], im.upto(d))
                wait(pe, v_ready, im.upto(d))
                if g == 2:
                    wait(pe, o_out[0], im.upto(d))
                elif g == 0:
                    wait(pe, o_out[1], im.upto(d - 1))
                else:
                    wait(pe, o_out[2], im.upto(d - 1))
                    wait(pe, attn_ready, im.upto(d - 1))
                dst = o_bank(s, g)
                for k in range(2):
                    for q in range(4):
                        h = 4 * g + q
                        last = pe.matmul(dst[HW * q:HW * (q + 1), 0:G], val[s][:, k, h], prob[h][:, k * G:(k + 1) * G],
                                         start=(k == 0), stop=(k == 1))
                last.then_inc(o_ready[g], 1)

            def turn_o(im, d):
                wait(pe, o_out[2], im.upto(d))
                wait(pe, h1_ready, im.upto(d - 1))
                for j, dst in enumerate((W, o_bank(im.slot(d), 2))):
                    for g in range(3):
                        last = pe.transpose(dst[0:T, g * 128:(g + 1) * 128], oT[:, g, j * T:(j + 1) * T], ident[:, :])
                last.then_inc(o_tokens, 1)

            def turn_a(im):
                wait(pe, attn_ready, im.upto(-1))
                wait(pe, gate_summed, im.upto(-2))
                turn(W, attn, aT_ready)

            def project_mm(im):
                wait(pe, aT_split, im.upto(-1))
                for j in range(2):
                    last = split_product(W[0:T, j * D:(j + 1) * D],
                                         lambda a, k: aT[:, a, k * G + j * T:k * G + (j + 1) * T],
                                         lambda b, k: proj_w[:, b, k], slice(0, D), NKC)
                last.then_inc(proj_ready, 1)

            def turn_y2(im, d):
                wait(pe, y2_ready, im.upto(d))
                if im.has(d + 1):
                    wait(pe, attn_ready, im.upto(d + 1))
                turn(W, y2, y2T_ready)

            pe.wait_ge(weights_ready, 1)
            zero = Image(pe, 0, 0)
            patches_mm(zero, 0, 0)
            patches_mm(zero, 0, 1)
            turn_y(zero, 0)
            queries_keys_mm(zero, 0, 0)
            queries_keys_mm(zero, 0, 1)
            values_mm(zero, 0)
            turn_qk(zero, 0, 0)
            turn_qk(zero, 0, 1)
            patches_mm(zero, 1, 0)
            patches_mm(zero, 1, 1)
            scores(zero, 0, 0)
            scores(zero, 0, 1)
            turn_y(zero, 1)
            scores(zero, 0, 2)

            def step(im, patches, prepare, project, finish):
                scores(im, 0, 3)
                scores(im, 0, 4)
                if prepare:
                    queries_keys_mm(im, 1, 0)
                    queries_keys_mm(im, 1, 1)
                    values_mm(im, 1)
                scores(im, 0, 5)
                if finish:
                    turn_y2(im, -2)
                if patches:
                    patches_mm(im, 2, 0)
                scores(im, 0, 6)
                if patches:
                    patches_mm(im, 2, 1)
                scores(im, 0, 7)
                weigh(im, 0, 0)
                if project:
                    turn_a(im)
                scores(im, 0, 8)
                weigh(im, 0, 1)
                scores(im, 0, 9)
                if prepare:
                    turn_qk(im, 1, 0)
                scores(im, 0, 10)
                if project:
                    project_mm(im)
                scores(im, 0, 11)
                if prepare:
                    scores(im, 1, 0)
                    turn_qk(im, 1, 1)
                weigh(im, 0, 2)
                if prepare:
                    scores(im, 1, 1)
                if patches:
                    turn_y(im, 2)
                if prepare:
                    scores(im, 1, 2)
                turn_o(im, 0)

            over_images(pe, step)
            last = Image(pe, B, 0)
            turn_y2(last, -2)
            turn_a(last)
            project_mm(last)
            turn_y2(last, -1)

            pe.wait_ge(gate_summed, B)
            pe.wait_ge(h1_ready, B)
            for k in range(NKC):
                last = pe.matmul(X[0:B, 0:E], gate_sum[:, :, k], gate_w[:, k], start=(k == 0), stop=(k == NKC - 1))
            last.then_inc(logits_ready, 1)
            pe.wait_ge(gate_wide, 1)
            for n in range(2):
                last = pe.matmul(Y[0:T, n * B:(n + 1) * B], g_wide[:, n], ident[0:B, 0:B], start=True, stop=True)
            last.then_inc(gate_ready, 1)

            def first_product(im, d, m):
                s = im.slot(d)
                n = im.index + d
                if m == 0:
                    wait(pe, w1_chosen, im.upto(d))
                    if isinstance(n, int):
                        wait(pe, x2_in[s], 16 * (n // 2 + 1))
                    else:
                        pe.wait_ge(x2_in[s], pe.snap((n - s) * 8 + 16))
                wait(pe, hid_act[m], im.upto(d - 1))
                for c in range(2):
                    f = (2 * m + c) * 128
                    rows = lambda k: KC + (k == NKC - 1)
                    last = split_product(bank[m][:, c * G:(c + 1) * G],
                                         lambda a, k: w1_sel[s][0:rows(k), a, k, f:f + 128],
                                         lambda b, k: x2[s][0:rows(k), b, k], slice(0, G), NKC)
                last.then_inc(hid_ready[m], 1)

            def second_product(im, m):
                s = im.slot(0)
                wait(pe, hid_split[m], im.upto(0))
                if m == 0:
                    wait(pe, w2_chosen, im.upto(0))
                    wait(pe, y_read, im.upto(-2))
                for c in range(2):
                    for j in range(2):
                        for n, (a, b) in enumerate(((0, 0), (0, 1), (1, 0))):
                            last = pe.matmul(bank[3 + 2 * s + j][0:T, 0:D],
                                             hidT[m][:, a, c * G + j * T:c * G + (j + 1) * T],
                                             w2_sel[s][:, b, 2 * m + c],
                                             start=(m == 0 and c == 0 and n == 0), stop=(m == 2 and c == 1 and n == 2))
                last.then_inc(hid_used[m], 1)

            zero = Image(pe, 0, 0)
            pe.wait_ge(rows_set, 4)
            pe.wait_ge(expert_known, 1)
            for m in range(3):
                first_product(zero, 0, m)

            def step_2(im, more):
                for m in range(3):
                    if more or im.index + 1 < B:
                        first_product(im, 1, m)
                    second_product(im, m)

            over_images_2(pe, step_2)



def kernel(x, L0_tok_gamma, L0_tok_beta, L0_tok_W, L0_tok_b, L0_attn_qkv_weight, L0_attn_proj_weight,
           L0_ffn_Wg, L0_ffn_W1, L0_ffn_b1, L0_ffn_W2, L0_ffn_b2):
    import numpy as np
    import concourse.bacc as bacc
    from concourse.bass_utils import run_bass_kernel_spmd

    x = np.asarray(x)
    B, C, H, W = x.shape
    R = H // PATCH
    parts = x.reshape(B, C, R, 2, HALF, R, 2, HALF).transpose(3, 6, 0, 4, 7, 1, 2, 5)
    own = np.ascontiguousarray(parts.transpose(2, 0, 3, 4, 5, 1, 6, 7)).reshape(B, 128, CH * 2, R * R)
    opposite = np.zeros((B, 2, HALF, HALF, C, 2, R + 1, R + 1), x.dtype)
    for a in range(2):
        for b in range(2):
            opposite[:, a, :, :, :, b, 1 - a:1 - a + R, 1 - b:1 - b + R] = parts[1 - a, 1 - b]
    opposite = opposite.reshape(B, 128, CH * 2 * (R + 1) * (R + 1))

    def by_pixel(v):
        v = np.asarray(v).reshape(-1, 2, HALF, 2, HALF, CH)
        return np.ascontiguousarray(v.transpose(1, 2, 4, 5, 3, 0)).reshape(128, CH * 2, -1)

    def by_chunk(v):
        v = np.asarray(v).T
        return np.ascontiguousarray(v.reshape(NKC, KC, -1).transpose(1, 0, 2))

    arrays = {
        "own": own, "opposite": opposite, "tok_W": by_pixel(L0_tok_W),
        "tok_gamma": by_pixel(L0_tok_gamma)[:, :, 0], "tok_beta": by_pixel(L0_tok_beta)[:, :, 0],
        "tok_b": np.asarray(L0_tok_b), "qkv_W": by_chunk(L0_attn_qkv_weight), "proj_W": by_chunk(L0_attn_proj_weight),
        "gate_W": by_chunk(L0_ffn_Wg), "W1": np.asarray(L0_ffn_W1), "b1": np.asarray(L0_ffn_b1),
        "W2": np.asarray(L0_ffn_W2), "b2": np.asarray(L0_ffn_b2),
    }
    arrays = {k: np.ascontiguousarray(v) for k, v in arrays.items()}
    nc = bacc.Bacc("TRN2", target_bir_lowering=False, num_devices=1, dynamic_dma_scratch_size=1024)
    args = [nc.dram_tensor(f"in_{k}", v.shape, mybir.dt.from_np(v.dtype), kind="ExternalInput").ap()
            for k, v in arrays.items()]
    out = nc.dram_tensor("out_0", (B, R * R, D), F32, kind="ExternalOutput").ap()
    build_vit(nc, *args, out)
    r = run_bass_kernel_spmd(nc, [{f"in_{k}": v for k, v in arrays.items()}], core_ids=[0])
    return r.results[0]["out_0"]
```

```python
from contextlib import ExitStack

import concourse.bass as bass
from concourse import mybir

F32 = mybir.dt.float32
F16 = mybir.dt.float16
I32 = mybir.dt.int32
ALU = mybir.AluOpType
ACT = mybir.ActivationFunctionType
AX_X = mybir.AxisListType.X

EPS = 1e-5
B1_HIGH, B1_LOW = 64, 96
PATCH = 16
HALF = PATCH // 2
CH = 3
D = 192
HEADS = 12
HD = D // HEADS
HW = 32
KC = 96
NKC = D // KC
LEAD, TAIL = 128, D - 128
E = 3
FF = 768
FC = FF // 128

S_X = 64.0
S_ACT = 32.0
S_W = 256.0
S_QK = 64.0
S_HID = 16.0

EPS_QK = HD * EPS * (S_ACT * S_W) ** 2
NEWTON = 3


class Image:

    images = 0

    def __init__(self, engine, index, position):
        self.engine, self.index, self.position, self.kept = engine, index, position, {}

    def upto(self, d):
        if isinstance(self.index, int):
            return self.index + d + 1
        if d not in self.kept:
            self.kept[d] = self.engine.snap(self.index + (d + 1))
        return self.kept[d]

    def has(self, d):
        return not isinstance(self.index, int) or self.index + d < self.images

    def stands_at(self, n):
        return isinstance(self.index, int) and self.index == n

    def slot(self, d, slots=2):
        return (self.position + d) % slots


def wait(engine, sem, count):
    if not isinstance(count, int) or count > 0:
        engine.wait_ge(sem, count)


def build_vit(nc, own, opposite, tokW, tokGamma, tokBeta, tokB, qkvW, projW, gateW, W1, b1, W2, b2, out):
    B = Image.images = own.shape[0]
    G = own.shape[3]
    CB = own.shape[2]
    SIDE = 14
    T = G // 2
    PD = CH * PATCH * PATCH
    OPP = SIDE + 1

    h1_dram = nc.dram_tensor("h1_scratch", [B, T, 2 * D], F32).ap()
    y2_dram = nc.dram_tensor("y2_scratch", [B, 128, 2 * NKC * G], F16).ap()

    with ExitStack() as ctx:
        def sem(name):
            return ctx.enter_context(nc.semaphore(name))

        WORDS = 54000
        arena = ctx.enter_context(nc.sbuf_tensor("arena", [128, WORDS], F32))
        used = [0]

        def take(parts, *dims, dt=F32):
            n = 1
            for x in dims:
                n *= x
            words = n if dt in (F32, I32) else (n + 1) // 2
            words = (words + 7) // 8 * 8
            at = used[0]
            used[0] += words
            assert used[0] <= WORDS, used[0]
            v = arena[0:parts, at:at + (n if dt in (F32, I32) else n // 2)]
            if dt != F32:
                v = v.bitcast(dt)
            if len(dims) > 1:
                names = [f"d{k}" for k in range(len(dims))]
                v = v.rearrange("p (" + " ".join(names) + ") -> p " + " ".join(names), **dict(zip(names, dims)))
            return v

        ident = take(128, 128)
        ident16 = take(128, 128, dt=F16)
        ones = take(128, 128)
        eps_ln = take(T, 2)
        eps_tok = take(T, 2)
        minus_half = take(T, 2)
        gate_w = take(128, NKC, E)
        token_sum = take(128, NKC)
        gate_sum = take(128, B, NKC)
        w1_all = take(128, E, 2, NKC * FF, dt=F16)
        w2_all = take(128, E, 2, FC * D, dt=F16)
        b2_all = take(T, E * D)
        x2 = [take(128, 2, NKC, G, dt=F16) for _ in range(4)]
        after_shared = used[0]

        tok_w = take(128, 2, CB, D + 1, dt=F16)
        tok_bias = take(T, D)
        qkv_w = take(KC, 2, NKC, 3 * D, dt=F16)
        proj_w = take(KC, 2, NKC, D, dt=F16)
        own_x = [take(128, CB * G) for _ in range(2)]
        opp_x = [take(128, CB, OPP, OPP) for _ in range(2)]
        row_sum = take(128, CB, SIDE, OPP)
        xcat = [take(128, CB, G) for _ in range(2)]
        x_halves = [take(128, 2, CB, G, dt=F16) for _ in range(4)]
        xsq = take(128, CB, G)
        xsq_sum = take(128, G)
        tok_mean = take(T, 2)
        tok_mean2 = take(T, 2)
        tok_var = take(T, 2)
        tok_rstd = take(T, 2)
        tok_sh, sh1, sh2 = take(T, 2), take(T, 2), take(T, 2)
        qk_var = take(T, 4 * HEADS)
        qk_t = take(T, 4 * HEADS)
        h0 = [take(T, 2, D) for _ in range(4)]
        y = take(T, 2, D)
        yT = take(KC, 2, NKC * G, dt=F16)
        bn1 = take(T, 2, 6)
        mv1 = take(T, 2, 2)
        rstd1 = take(T, 2)
        qk_sq = take(T, 2, 2 * HEADS, HD + 1)
        qk_rs = take(T, 4 * HEADS)
        qk_n = take(T, 2, 2 * HEADS, HD)
        q_st = take(T, 2 * HEADS, 4 * HD, dt=F16)
        k_st = take(T, 2 * HEADS, 4 * HD, dt=F16)
        qT = [take(128, HEADS // 2, G, dt=F16) for _ in range(2)]
        kT = [take(128, HEADS // 2, G, dt=F16) for _ in range(2)]
        val = [take(T, 2, HEADS, HW) for _ in range(2)]
        prob = [take(T, 2 * G) for _ in range(HEADS)]
        oT = take(128, 3, G)
        rden = take(T, 2, HEADS)
        attn = take(T, 2, D)
        aT = take(KC, 2, NKC * G, dt=F16)
        h1 = [take(T, 2, D) for _ in range(2)]
        bn2 = take(T, 2, 6)
        mv2 = take(T, 2, 2)
        rstd2 = take(T, 2)
        y2 = take(T, 2, D)
        y2T = [take(128, 2, 2, G, dt=F16) for _ in range(2)]
        after_images = used[0]
        tok_raw = take(128, CB, D)
        tok_full = take(128, CB, D + 1)
        tok_gam = take(128, CB)
        tok_bet = take(128, CB)
        beta_cols = take(128, CB, T)
        tok_b = take(T, D)
        qkv_raw = take(KC, NKC, 3 * D)
        qkv_gs = take(KC, NKC, 2 * HEADS)
        proj_raw = take(KC, NKC, D)

        used[0] = after_images
        w1_raw = take(128, NKC, FF)
        b1_raw = take(B1_LOW + 1, E, FF)
        w2_raw = take(128, FC, D)

        used[0] = after_shared
        w1_sel = [take(128, 2, NKC, FF, dt=F16) for _ in range(2)]
        w2_sel = [take(128, 2, FC, D, dt=F16) for _ in range(2)]
        h1_in = [take(T, 2, D) for _ in range(2)]
        hid = [take(128, 2 * G) for _ in range(3)]
        hidT = [take(128, 2, 2 * G, dt=F16) for _ in range(3)]
        y_out = [take(T, 2, D) for _ in range(2)]
        y_fin = [take(T, 2, D) for _ in range(2)]
        g_logit = take(B, E)
        g_max = take(B, 1)
        g_sub = take(B, E)
        g_exp = take(B, E)
        g_sum = take(B, 1)
        g_pair = take(B, 2)
        g_is = take(B, E)
        g_not = take(B, 2)
        g_wide = take(B, 2, T)
        gate = take(T, B)
        expert = take(1, B, dt=I32)

        bank = [ctx.enter_context(nc.psum_tensor(f"bank{n}", [128, 512], F32)) for n in range(8)]
        S = bank[0:2]
        O = bank[2:4]
        W = bank[4]
        X, Y, Z = bank[5:8]
        Y16, Z16 = Y[:, :].bitcast(F16), Z[:, :].bitcast(F16)

        def o_bank(image_slot, g):
            return O[(image_slot + g) % 2]

        tok_in = sem("tok_in")
        weights_in = sem("weights_in")
        const_ready = sem("const_ready")
        blanks_ready = sem("blanks_ready")
        setup_dve = sem("setup_dve")
        setup_mm = sem("setup_mm")
        patch_weights_ready = sem("patch_weights_ready")
        weights_ready = sem("weights_ready")
        x_in = [sem(f"x_in{n}") for n in range(2)]
        rows_added = sem("rows_added")
        cols_added = sem("cols_added")
        xcat_ready = sem("xcat_ready")
        x_high = sem("x_high")
        x_split = sem("x_split")
        xsq_ready = sem("xsq_ready")
        xsq_fold = [sem(f"xsq_fold{n}") for n in range(2)]
        xsq_summed = sem("xsq_summed")
        tok_ready = sem("tok_ready")
        tok_stat = [sem(f"tok_stat{n}") for n in range(4)]
        h0_ready = sem("h0_ready")
        ln1_stat = [sem(f"ln1_stat{n}") for n in range(3)]
        y_ready = sem("y_ready")
        yT_ready = sem("yT_ready")
        yT_high = sem("yT_high")
        yT_split = sem("yT_split")
        qk_ready = [sem(f"qk_ready{j}") for j in range(2)]
        v_product = sem("v_product")
        qk_squared = [sem(f"qk_squared{j}") for j in range(2)]
        qk_summed = [sem(f"qk_summed{j}") for j in range(2)]
        qk_step = [sem(f"qk_step{n}") for n in range(3 * NEWTON + 1)]
        tok_shifted, ln1_shifted, ln2_shifted = (sem(f"{n}_shifted") for n in ("tok", "ln1", "ln2"))
        qk_normed = sem("qk_normed")
        qk_high = [sem(f"{n}_high") for n in "qk"]
        qk_split = [sem(f"{n}_split") for n in "qk"]
        v_ready = sem("v_ready")
        stack_T = [sem(f"stack_T{r}") for r in range(2)]
        q_ready = [sem(f"q_ready{r}") for r in range(2)]
        k_ready = [sem(f"k_ready{r}") for r in range(2)]
        scores_ready = [sem(f"scores_ready{h}") for h in range(HEADS)]
        prob_ready = [sem(f"prob_ready{h}") for h in range(HEADS)]
        o_ready = [sem(f"o_ready{g}") for g in range(3)]
        o_out = [sem(f"o_out{g}") for g in range(3)]
        o_tokens = sem("o_tokens")
        den_inv = sem("den_inv")
        attn_ready = sem("attn_ready")
        aT_ready = sem("aT_ready")
        aT_high = sem("aT_high")
        aT_split = sem("aT_split")
        proj_ready = sem("proj_ready")
        h1_ready = sem("h1_ready")
        ln2_stat = [sem(f"ln2_stat{n}") for n in range(3)]
        y2_ready = sem("y2_ready")
        y2T_ready = sem("y2T_ready")
        y2T_high = sem("y2T_high")
        y2T_split = sem("y2T_split")
        gate_summed = sem("gate_summed")
        h1_saved = [sem(f"h1_saved{n}") for n in range(2)]
        y2_saved = [sem(f"y2_saved{n}") for n in range(2)]

        experts_in = sem("experts_in")
        rows_set = sem("rows_set")
        high_taken = sem("high_taken")
        low_taken = sem("low_taken")
        b1_high = sem("b1_high")
        b1_low = sem("b1_low")
        stacked = sem("stacked")
        logits_ready = sem("logits_ready")
        gate_step = sem("gate_step")
        gate_exp = sem("gate_exp")
        gate_wide = sem("gate_wide")
        gate_ready = sem("gate_ready")
        expert_known = sem("expert_known")
        x2_in = [sem(f"x2_in{n}") for n in range(4)]
        h1_back = [sem(f"h1_back{n}") for n in range(2)]
        w1_chosen = sem("w1_chosen")
        w2_chosen = sem("w2_chosen")
        hid_ready = [sem(f"hid_ready{m}") for m in range(3)]
        hid_act = [sem(f"hid_act{m}") for m in range(3)]
        hid_high = [sem(f"hid_high{m}") for m in range(3)]
        hid_split = [sem(f"hid_split{m}") for m in range(3)]
        hid_used = [sem(f"hid_used{m}") for m in range(3)]
        y_read = sem("y_read")
        y_done = sem("y_done")
        y_saved = [sem(f"y_saved{n}") for n in range(2)]

        block = ctx.enter_context(nc.Block())

        CONSTS = 5
        BLANKS = 6
        assert B % 4 == 0
        TURNS = (B - 12) // 4
        TURNS_2 = (B - 8) // 4

        def over_images(engine, step):
            for n in range(4):
                step(Image(engine, n, n), True, True, n > 0, n > 1)
            with engine.Fori(0, TURNS) as turn:
                for n in range(4):
                    step(Image(engine, engine.snap(turn * 4 + (n + 4)), n), True, True, True, True)
            for n in range(B - 8, B):
                step(Image(engine, n, n % 4), n + 2 < B, n + 1 < B, True, True)

        def over_images_2(engine, step):
            step(Image(engine, 0, 0), True)
            step(Image(engine, 1, 1), True)
            with engine.Fori(0, TURNS_2) as turn:
                for n in range(2, 6):
                    step(Image(engine, engine.snap(turn * 4 + n), n % 4), True)
            for n in range(B - 6, B):
                step(Image(engine, n, n % 4), n + 2 < B)

        @block.sync
        def _(sp):
            def load_x(im, d):
                s = im.slot(d)
                wait(sp, rows_added, im.upto(d - 2))
                wait(sp, xcat_ready, im.upto(d - 2))
                n = im.index + d
                n = slice(n, n + 1) if isinstance(n, int) else bass.ds(n, 1)
                sp.dma_start(opp_x[s].rearrange("p a b c -> p (a b c)"),
                             opposite[n].rearrange("o p f -> (o p) f")).then_inc(x_in[s], 16)
                sp.dma_start(own_x[s], own[n].rearrange("o p c g -> (o p) (c g)")).then_inc(x_in[s], 16)

            def save_h1(im, d):
                s = im.slot(d)
                n = im.index + d
                n = slice(n, n + 1) if isinstance(n, int) else bass.ds(n, 1)
                wait(sp, h1_ready, im.upto(d))
                sp.dma_start(h1_dram[n].rearrange("o p f -> (o p) f"),
                             h1[s].rearrange("p a b -> p (a b)")).then_inc(h1_saved[s], 16)

            def save_y2(im, d):
                s = im.slot(d)
                n = im.index + d
                n = slice(n, n + 1) if isinstance(n, int) else bass.ds(n, 1)
                wait(sp, y2T_split, im.upto(d))
                for rows, src_rows, cols in ((slice(0, TAIL), slice(0, TAIL), slice(0, 2 * G)),
                                             (slice(0, TAIL), slice(TAIL, 128), slice(2 * G, 4 * G)),
                                             (slice(TAIL, 128), slice(TAIL, 128), slice(0, 4 * G))):
                    sp.dma_start(y2_dram[n, rows, cols].rearrange("o p f -> (o p) f"),
                                 y2T[s][src_rows].rearrange("p k a g -> p (k a g)")[:, cols]).then_inc(y2_saved[s], 16)

            def load_expert(e):
                wait(sp, low_taken, e)
                sp.dma_start(w1_raw, W1[e]).then_inc(experts_in, 16)
                sp.dma_start(w2_raw, W2[e].rearrange("(c p) d -> p c d", c=FC)).then_inc(experts_in, 16)

            zero = Image(sp, 0, 0)
            sp.dma_start(tok_gam, tokGamma).then_inc(tok_in, 16)
            sp.dma_start(tok_raw, tokW).then_inc(tok_in, 16)
            sp.dma_start(tok_bet, tokBeta).then_inc(tok_in, 16)
            load_x(zero, 0)
            sp.dma_start(tok_b, tokB.partition_broadcast(T)).then_inc(weights_in, 16)
            sp.dma_start(qkv_raw, qkvW).then_inc(weights_in, 16)
            sp.dma_start(proj_raw, projW).then_inc(weights_in, 16)
            sp.dma_start(gate_w, gateW).then_inc(weights_in, 16)
            for d in range(1, 6):
                load_x(zero, d)
            sp.wait_ge(weights_ready, 1)
            sp.dma_start(b1_raw[B1_HIGH:B1_LOW + 1], b1.partition_broadcast(B1_LOW + 1 - B1_HIGH)).then_inc(experts_in, 16)
            sp.dma_start(b2_all, b2.rearrange("e d -> (e d)").partition_broadcast(T)).then_inc(experts_in, 16)
            load_expert(0)

            def step(im, patches, prepare, project, finish):
                if im.has(6):
                    load_x(im, 6)
                if finish:
                    save_y2(im, -2)
                if project:
                    save_h1(im, -1)
                if im.stands_at(B - 4):
                    load_expert(1)
                if im.stands_at(B - 3):
                    load_expert(2)

            over_images(sp, step)
            last = Image(sp, B, 0)
            save_y2(last, -2)
            save_h1(last, -1)
            save_y2(last, -1)
            for s in range(2):
                sp.wait_ge(h1_saved[s], 16 * (B // 2))
                sp.wait_ge(y2_saved[s], 48 * (B // 2))
            sp.wait_ge(gate_summed, B)
            sp.wait_ge(o_ready[2], B)

            def load_normed(im, d):
                s = im.slot(d, 4)
                n = im.index + d
                n = slice(n, n + 1) if isinstance(n, int) else bass.ds(n, 1)
                wait(sp, hid_ready[2], im.upto(d - 4))
                for rows, cols in ((slice(0, TAIL), 4 * G), (slice(TAIL, 128), 3 * G)):
                    sp.dma_start(x2[s][rows].rearrange("p k a g -> p (k a g)")[:, 0:cols],
                                 y2_dram[n, rows, 0:cols].rearrange("o p f -> (o p) f")).then_inc(x2_in[s], 16)

            def load_h1(im, d):
                s = im.slot(d)
                n = im.index + d
                n = slice(n, n + 1) if isinstance(n, int) else bass.ds(n, 1)
                wait(sp, y_done, im.upto(d - 2))
                sp.dma_start(h1_in[s].rearrange("p a b -> p (a b)"),
                             h1_dram[n].rearrange("o p f -> (o p) f")).then_inc(h1_back[s], 16)

            zero = Image(sp, 0, 0)
            for d in range(2):
                load_normed(zero, d)
                load_h1(zero, d)
            load_normed(zero, 2)

            def step_2(im, more):
                s = im.slot(0)
                if im.has(3):
                    load_normed(im, 3)
                wait(sp, y_done, im.upto(0))
                n = im.index
                n = slice(n, n + 1) if isinstance(n, int) else bass.ds(n, 1)
                sp.dma_start(out[n].rearrange("o (j p) d -> p (o j) d", j=2), y_fin[s]).then_inc(y_saved[s], 16)
                if more:
                    load_h1(im, 2)

            over_images_2(sp, step_2)
            for s in range(2):
                sp.wait_ge(y_saved[s], 16 * (B // 2))

        @block.gpsimd
        def _(pool):
            pool.memset(ones, 1.0)
            pool.memset(eps_ln, EPS)
            pool.memset(eps_tok, EPS * (S_X * S_W) ** 2)
            pool.memset(minus_half, -0.5)
            pool.memset(qk_sq, EPS_QK)
            pool.memset(ident, 0.0).then_inc(const_ready, 1)
            pool.memset(ident16, 0.0).then_inc(const_ready, 1)
            pool.wait_ge(const_ready, 2)
            for m in (ident, ident16):
                pool.affine_select(out=m, in_=m, compare_op=ALU.not_equal, fill=1.0, base=0,
                                   pattern=[[-1, 128]], channel_multiplier=1).then_inc(const_ready, 1)
            pool.memset(tok_full[:, :, D:D + 1], 1.0).then_inc(const_ready, 1)

            def add_rows(im, d):
                s = im.slot(d)
                n = im.index + d
                if isinstance(n, int):
                    wait(pool, x_in[s], 32 * (n // 2 + 1))
                else:
                    pool.wait_ge(x_in[s], pool.snap((n - s) * 16 + 32))
                wait(pool, cols_added, im.upto(d - 1))
                pool.tensor_tensor(row_sum, opp_x[s][:, :, 0:SIDE, :], opp_x[s][:, :, 1:OPP, :],
                                   ALU.add).then_inc(rows_added, 1)

            def add_cols(im, d):
                s = im.slot(d)
                wait(pool, rows_added, im.upto(d))
                wait(pool, xsq_ready, im.upto(d - 2))
                wait(pool, x_split, im.upto(d - 2))
                rows = row_sum.rearrange("p c r q -> p (c r) q")
                pool.tensor_tensor(xcat[s].rearrange("p c (r q) -> p (c r) q", q=SIDE),
                                   rows[:, :, 0:SIDE], rows[:, :, 1:OPP], ALU.add).then_inc(cols_added, 1)

            def add_own(im, d):
                s = im.slot(d)
                wait(pool, cols_added, im.upto(d))
                flat = xcat[s].rearrange("p c g -> p (c g)")
                pool.tensor_tensor(flat, flat, own_x[s], ALU.add).then_inc(xcat_ready, 1)

            def pixel_sums(im, d):
                add_rows(im, d)
                add_cols(im, d)
                add_own(im, d)

            def inverse_root(dst, shifted, src, eps, ready, step, done, im, d):
                wait(pool, ready, im.upto(d))
                pool.tensor_tensor(shifted, src, eps, ALU.add).then_inc(step, 1)
                wait(pool, step, im.upto(d))
                pool.tensor_tensor(dst, shifted, minus_half, ALU.pow).then_inc(done, 1)

            def root_tokens(im, d):
                inverse_root(tok_rstd, tok_sh, tok_var, eps_tok, tok_stat[2], tok_shifted, tok_stat[3], im, d)

            def root_normed_tokens(im, d):
                inverse_root(rstd1, sh1, mv1[:, :, 1], eps_ln, ln1_stat[1], ln1_shifted, ln1_stat[2], im, d)

            def root_h1(im):
                inverse_root(rstd2, sh2, mv2[:, :, 1], eps_ln, ln2_stat[1], ln2_shifted, ln2_stat[2], im, -1)

            def sum_squares(im, d):
                wait(pool, tok_ready, im.upto(d - 1))
                wait(pool, xsq_ready, im.upto(d))
                pool.tensor_tensor(xsq[:, 0:3], xsq[:, 0:3], xsq[:, 3:6], ALU.add).then_inc(xsq_fold[0], 1)
                wait(pool, xsq_fold[0], im.upto(d))
                pool.tensor_tensor(xsq[:, 0], xsq[:, 0], xsq[:, 1], ALU.add).then_inc(xsq_fold[1], 1)
                wait(pool, xsq_fold[1], im.upto(d))
                pool.tensor_tensor(xsq_sum, xsq[:, 0], xsq[:, 2], ALU.add).then_inc(xsq_summed, 1)

            def expert_stack(e):
                tail = slice(FF, 2 * FF)
                pool.wait_ge(high_taken, e + 1)
                pool.tensor_copy(w1_all[0:TAIL, e, 1, tail], w1_all[0:TAIL, e, 0, tail]).then_inc(stacked, 1)

            zero = Image(pool, 0, 0)
            pixel_sums(zero, 0)
            sum_squares(zero, 0)
            add_rows(zero, 1)
            root_tokens(zero, 0)
            root_normed_tokens(zero, 0)
            add_cols(zero, 1)
            add_own(zero, 1)
            pixel_sums(zero, 2)
            sum_squares(zero, 1)
            add_rows(zero, 3)
            root_tokens(zero, 1)
            add_cols(zero, 3)
            root_normed_tokens(zero, 1)
            add_own(zero, 3)
            sum_squares(zero, 2)
            pixel_sums(zero, 4)

            def step(im, patches, prepare, project, finish):
                if patches:
                    root_tokens(im, 2)
                    root_normed_tokens(im, 2)
                if im.has(5):
                    add_rows(im, 5)
                if project:
                    root_h1(im)
                if im.has(5):
                    add_cols(im, 5)
                if im.has(3):
                    sum_squares(im, 3)
                if im.has(5):
                    add_own(im, 5)

                if im.stands_at(B - 3):
                    expert_stack(0)
                if im.stands_at(B - 2):
                    expert_stack(1)

            over_images(pool, step)
            expert_stack(2)
            root_h1(Image(pool, B, 0))

        @block.scalar
        def _(act):
            def square_x(im, d):
                s = im.slot(d)
                wait(act, xcat_ready, im.upto(d))
                wait(act, xsq_summed, im.upto(d - 1))
                act.activation(xsq, xcat[s], ACT.Square).then_inc(xsq_ready, 1)

            def high_x(im, d):
                wait(act, xcat_ready, im.upto(d))
                wait(act, tok_ready, im.upto(d - 4))
                act.activation(x_halves[im.slot(d, 4)][:, 0], xcat[im.slot(d)], ACT.Copy, scale=S_X).then_inc(x_high, 1)

            def high(psum, dst, ready, prev_used, done, im, d):
                wait(act, ready, im.upto(d))
                for sem_, n in prev_used:
                    wait(act, sem_, n)
                act.activation(dst[:, 0], psum[0:KC, 0:NKC * G], ACT.Copy, scale=S_ACT).then_inc(done, 1)

            def high_y(im, d):
                high(X, yT, yT_ready, [(v_product, im.upto(d - 1))], yT_high, im, d)

            def square_qk(im, d, j):
                wait(act, qk_ready[j], im.upto(d))
                wait(act, qk_summed[j], im.upto(d - 1))
                act.activation(qk_sq[:, j, :, 0:HD], (Y, Z)[j][0:T, 0:2 * D].rearrange("p (h e) -> p h e", e=HD),
                               ACT.Square).then_inc(qk_squared[j], 1)

            def high_qk(im, d, n):
                dst, blocks = ((q_st, slice(0, 3, 2)), (k_st, slice(0, 2)))[n]
                wait(act, qk_normed, im.upto(d))
                wait(act, stack_T[1], im.upto(d - 1))
                act.activation(dst.rearrange("p h (b e) -> p h b e", b=4)[:, :, blocks, :],
                               qk_n[:, n].unsqueeze(2).to_broadcast([T, 2 * HEADS, 2, HD]), ACT.Copy,
                               scale=S_QK).then_inc(qk_high[n], 1)

            def values(im, d):
                s = im.slot(d)
                wait(act, v_product, im.upto(d))
                wait(act, o_ready[2], im.upto(d - 2))
                act.activation(val[s][:, :, :, 0:HD].rearrange("p k h e -> p (k h) e"),
                               X[0:T, 0:2 * D].rearrange("p (h e) -> p h e", e=HD),
                               ACT.Copy, scale=1.0 / (S_ACT * S_W)).then_inc(v_ready, 1)

            def keys(im, d, r):
                s = im.slot(d)
                wait(act, stack_T[r], im.upto(d))
                wait(act, scores_ready[HEADS - 1], im.upto(d - 2))
                act.copy(kT[s][:, 3 * r:3 * r + 3, :].rearrange("p h g -> p (h g)"),
                         Y16[:, 0:3 * G]).then_inc(k_ready[r], 1)

            def exps(im, d, h):
                wait(act, scores_ready[h], im.upto(d))
                wait(act, o_ready[h // 4], im.upto(d - 1))
                act.activation(prob[h], S[h % 2][0:T, 0:2 * G], ACT.Exp,
                               scale=HD ** 0.5 / (S_QK * S_QK)).then_inc(prob_ready[h], 1)

            def o_copy(im, d, g):
                wait(act, o_ready[g], im.upto(d))
                wait(act, o_tokens, im.upto(d - 1))
                act.copy(oT[:, g, :], o_bank(im.slot(d), g)[:, 0:G]).then_inc(o_out[g], 1)

            def high_a(im):
                high(W, aT, aT_ready, [(proj_ready, im.upto(-2))], aT_high, im, -1)

            def high_y2(im, d):
                n = im.index + d
                s = im.slot(d)
                if isinstance(n, int):
                    prev = [(y2_saved[s], 48 * (n // 2))]
                else:
                    prev = [(y2_saved[s], act.snap((n - s) * 24))]
                wait(act, y2T_ready, im.upto(d))
                for sem_, count in prev:
                    wait(act, sem_, count)
                wait(act, gate_summed, im.upto(d - 1))
                for k in range(NKC):
                    last = act.activation(y2T[s][:, k, 0], W[:, k * G:(k + 1) * G], ACT.Copy,
                                          scale=S_ACT, accum_out=token_sum[:, k:k + 1])
                last.then_inc(y2T_high, 1)

            def expert_high(e):
                act.wait_ge(experts_in, 16 * (2 * e + 4))
                act.activation(w1_all[:, e, 0], w1_raw.rearrange("p k f -> p (k f)"), ACT.Copy, scale=S_W)
                act.activation(w2_all[:, e, 0], w2_raw.rearrange("p c d -> p (c d)"), ACT.Copy,
                               scale=S_W).then_inc(high_taken, 1)

            zero = Image(act, 0, 0)
            high_x(zero, 0)
            square_x(zero, 0)
            high_y(zero, 0)
            square_qk(zero, 0, 0)
            square_qk(zero, 0, 1)
            act.wait_ge(blanks_ready, BLANKS)
            values(zero, 0)
            high_x(zero, 1)
            square_x(zero, 1)
            high_qk(zero, 0, 0)
            high_qk(zero, 0, 1)
            keys(zero, 0, 0)
            keys(zero, 0, 1)
            exps(zero, 0, 0)
            exps(zero, 0, 1)
            high_x(zero, 2)
            square_x(zero, 2)
            high_y(zero, 1)
            exps(zero, 0, 2)
            high_x(zero, 3)

            def step(im, patches, prepare, project, finish):
                exps(im, 0, 3)
                if prepare:
                    square_qk(im, 1, 0)
                exps(im, 0, 4)
                if prepare:
                    square_qk(im, 1, 1)
                    values(im, 1)
                exps(im, 0, 5)
                if finish:
                    high_y2(im, -2)
                if im.has(3):
                    square_x(im, 3)
                exps(im, 0, 6)
                exps(im, 0, 7)
                if prepare:
                    high_qk(im, 1, 0)
                    high_qk(im, 1, 1)
                if project:
                    high_a(im)
                exps(im, 0, 8)
                exps(im, 0, 9)
                o_copy(im, 0, 0)
                o_copy(im, 0, 1)
                if im.has(4):
                    high_x(im, 4)
                if prepare:
                    keys(im, 1, 0)
                exps(im, 0, 10)
                exps(im, 0, 11)
                if prepare:
                    keys(im, 1, 1)
                    exps(im, 1, 0)
                o_copy(im, 0, 2)
                if prepare:
                    exps(im, 1, 1)
                if patches:
                    high_y(im, 2)
                if prepare:
                    exps(im, 1, 2)
                if im.stands_at(B - 4):
                    expert_high(0)
                if im.stands_at(B - 3):
                    expert_high(1)
                if im.stands_at(B - 2):
                    expert_high(2)

            over_images(act, step)
            last = Image(act, B, 0)
            high_y2(last, -2)
            high_a(last)
            high_y2(last, -1)

            act.wait_ge(gate_step, 3)
            act.activation(g_exp, g_sub, ACT.Exp).then_inc(gate_exp, 1)

            def hidden(im, d):
                for m in range(3):
                    wait(act, hid_ready[m], im.upto(d))
                    wait(act, hid_split[m], im.upto(d - 1))
                    act.activation(hid[m], bank[m][:, 0:2 * G], ACT.Gelu,
                                   scale=1.0 / (S_ACT * S_W)).then_inc(hid_act[m], 1)
                    wait(act, hid_act[m], im.upto(d))
                    wait(act, hid_used[m], im.upto(d - 1))
                    act.activation(hidT[m][:, 0], hid[m], ACT.Copy, scale=S_HID).then_inc(hid_high[m], 1)

            hidden(Image(act, 0, 0), 0)

            def step_2(im, more):
                if more or im.index + 1 < B:
                    hidden(im, 1)

            over_images_2(act, step_2)

        @block.vector
        def _(dve):
            done = [0]

            def self_step(ins):
                done[0] += 1
                ins.then_inc(setup_dve, 1)
                dve.wait_ge(setup_dve, done[0])

            dve.wait_ge(tok_in, 16 * 3)
            dve.wait_ge(const_ready, CONSTS)
            self_step(dve.tensor_tensor(tok_full[:, :, 0:D], tok_raw,
                                        tok_gam.unsqueeze(2).to_broadcast([128, CB, D]), ALU.mult))
            self_step(dve.tensor_copy(beta_cols, tok_bet.unsqueeze(2).to_broadcast([128, CB, T])))
            for s in range(2):
                dve.memset(val[s], 0.0).then_inc(blanks_ready, 1)
            for blank in (q_st, k_st):
                dve.memset(blank, 0.0).then_inc(blanks_ready, 1)
            dve.wait_ge(blanks_ready, BLANKS - 2)
            for s in range(2):
                dve.memset(val[s][:, :, :, HD:HD + 1], 1.0).then_inc(blanks_ready, 1)

            for s in range(4):
                dve.memset(x2[s][TAIL:128, 1, 1], 0.0).then_inc(rows_set, 1)
            dve.wait_ge(rows_set, 4)
            for s in range(4):
                for row in (B1_HIGH, B1_LOW):
                    dve.memset(x2[s][row:row + 1, 1, 1], S_ACT).then_inc(rows_set, 1)

            dve.wait_ge(setup_mm, 1)
            self_step(dve.scalar_tensor_tensor(
                tok_full[:, :, 0:D], X[:, 0:D].unsqueeze(1).to_broadcast([128, CB, D]), -1.0 / PD,
                tok_full[:, :, 0:D], ALU.mult, ALU.add))
            self_step(dve.tensor_scalar(tok_w[:, 0], tok_full, S_W, None, ALU.mult))
            self_step(dve.scalar_tensor_tensor(tok_w[:, 1], tok_full, S_W, tok_w[:, 0], ALU.mult, ALU.subtract))
            dve.wait_ge(weights_in, 16 * 4)
            dve.tensor_tensor(tok_bias, Y[0:T, 0:D], tok_b, ALU.add).then_inc(patch_weights_ready, 1)

            def low_x(im, d, c=None):
                s = im.slot(d, 4)
                if not c:
                    wait(dve, x_high, im.upto(d))
                cs = slice(0, CB) if c is None else slice(c, c + 1)
                last = dve.scalar_tensor_tensor(x_halves[s][:, 1, cs], xcat[im.slot(d)][:, cs], S_X,
                                                x_halves[s][:, 0, cs], ALU.mult, ALU.subtract)
                if c is None or c == CB - 1:
                    last.then_inc(x_split, 1)

            def norm_stats(src, src_ready, bn, mv, steps, im, d):
                wait(dve, src_ready, im.upto(d))
                for j in range(2):
                    last = dve.bn_stats(bn[:, j], src[:, j])
                last.then_inc(steps[0], 1)
                dve.wait_ge(weights_ready, 1)
                wait(dve, steps[0], im.upto(d))
                for j in range(2):
                    last = dve.bn_aggr(mv[:, j], bn[:, j])
                last.then_inc(steps[1], 1)

            def norm_apply(src, dst, mv, rstd, steps, dst_ready, im, d):
                wait(dve, steps[2], im.upto(d))
                for j in range(2):
                    last = dve.tensor_scalar(dst[:, j], src[:, j], mv[:, j, 0:1], rstd[:, j:j + 1],
                                             ALU.subtract, ALU.mult)
                last.then_inc(dst_ready, 1)

            def token_stats(im, d):
                wait(dve, tok_ready, im.upto(d))
                sums = X[0:T, D:2 * (D + 1):D + 1]
                dve.tensor_scalar(tok_mean, sums, 1.0 / PD, None, ALU.mult).then_inc(tok_stat[0], 1)
                wait(dve, tok_stat[0], im.upto(d))
                dve.scalar_tensor_tensor(tok_mean2, sums, 1.0 / PD, tok_mean, ALU.mult, ALU.mult).then_inc(tok_stat[1], 1)
                wait(dve, tok_stat[1], im.upto(d))
                dve.scalar_tensor_tensor(tok_var, X[0:T, 2 * (D + 1):2 * (D + 1) + 2], (S_X * S_W) ** 2 / PD, tok_mean2,
                                         ALU.mult, ALU.subtract).then_inc(tok_stat[2], 1)

            def tokens(im, d):
                wait(dve, tok_stat[3], im.upto(d))
                wait(dve, h1_ready, im.upto(d - 4))
                for j in range(2):
                    last = dve.scalar_tensor_tensor(h0[im.slot(d, 4)][:, j], X[0:T, j * (D + 1):j * (D + 1) + D],
                                                    tok_rstd[:, j:j + 1], tok_bias, ALU.mult, ALU.add)
                last.then_inc(h0_ready, 1)

            def stats_tokens(im, d):
                norm_stats(h0[im.slot(d, 4)], h0_ready, bn1, mv1, ln1_stat, im, d)

            def norm_tokens(im, d):
                wait(dve, yT_ready, im.upto(d - 1))
                norm_apply(h0[im.slot(d, 4)], y, mv1, rstd1, ln1_stat, y_ready, im, d)

            def low(psum, dst, high_done, split, im, d):
                wait(dve, high_done, im.upto(d))
                dve.scalar_tensor_tensor(dst[:, 1], psum[0:KC, 0:NKC * G], S_ACT, dst[:, 0],
                                         ALU.mult, ALU.subtract).then_inc(split, 1)

            def sum_qk(im, d, j):
                wait(dve, qk_squared[j], im.upto(d))
                dve.tensor_reduce(qk_var[:, j * 2 * HEADS:(j + 1) * 2 * HEADS], qk_sq[:, j], AX_X,
                                  ALU.add).then_inc(qk_summed[j], 1)

            def norm_qk(im, d, ahead=False):
                wait(dve, qk_summed[0], im.upto(d))
                wait(dve, qk_summed[1], im.upto(d))
                dve.tensor_scalar(qk_rs.bitcast(I32), qk_var.bitcast(I32), -0.5, float(0x5F3759DF),
                                  ALU.mult, ALU.add).then_inc(qk_step[0], 1)
                for n in range(NEWTON):
                    if ahead:
                        low_x(im, 3, 2 * n)
                    wait(dve, qk_step[3 * n + 0], im.upto(d))
                    dve.scalar_tensor_tensor(qk_t, qk_rs, -0.5, qk_rs, ALU.mult, ALU.mult).then_inc(qk_step[3 * n + 1], 1)
                    wait(dve, qk_step[3 * n + 1], im.upto(d))
                    dve.tensor_tensor(qk_t, qk_t, qk_var, ALU.mult).then_inc(qk_step[3 * n + 2], 1)
                    if ahead:
                        low_x(im, 3, 2 * n + 1)
                    wait(dve, qk_step[3 * n + 2], im.upto(d))
                    dve.scalar_tensor_tensor(qk_rs, qk_t, 1.5, qk_rs, ALU.add, ALU.mult).then_inc(qk_step[3 * n + 3], 1)
                wait(dve, qk_step[3 * NEWTON], im.upto(d))
                wait(dve, qk_high[1], im.upto(d - 1))
                for j in range(2):
                    rs = qk_rs[:, j * 2 * HEADS:(j + 1) * 2 * HEADS].rearrange("p (a h) -> p a h", a=2)
                    last = dve.tensor_tensor(
                        qk_n[:, :, j * HEADS:(j + 1) * HEADS, :],
                        (Y, Z)[j][0:T, 0:2 * D].rearrange("p (a h e) -> p a h e", a=2, e=HD),
                        rs.unsqueeze(3).to_broadcast([T, 2, HEADS, HD]), ALU.mult)
                last.then_inc(qk_normed, 1)

            def low_qk(im, d, n):
                dst, block = ((q_st, 1), (k_st, 2))[n]
                wait(dve, qk_high[n], im.upto(d))
                dve.scalar_tensor_tensor(dst[:, :, block * HD:(block + 1) * HD], qk_n[:, n], S_QK, dst[:, :, 0:HD],
                                         ALU.mult, ALU.subtract).then_inc(qk_split[n], 1)

            def queries(im, d, r):
                s = im.slot(d)
                wait(dve, stack_T[r], im.upto(d))
                wait(dve, scores_ready[HEADS - 1], im.upto(d - 2))
                dve.tensor_copy(qT[s][:, 3 * r:3 * r + 3, :].rearrange("p h g -> p (h g)"),
                                Z16[:, 0:3 * G]).then_inc(q_ready[r], 1)

            def norm_attn(im, d):
                wait(dve, o_tokens, im.upto(d))
                wait(dve, aT_ready, im.upto(d - 1))
                src = [t[0:T, 0:3 * 128].rearrange("p (h w) -> p h w", w=HW)
                       for t in (W, o_bank(im.slot(d), 2))]
                for j in range(2):
                    last = dve.reciprocal(rden[:, j], src[j][:, :, HD])
                last.then_inc(den_inv, 1)
                wait(dve, den_inv, im.upto(d))
                for j in range(2):
                    last = dve.tensor_tensor(attn[:, j].rearrange("p (h e) -> p h e", e=HD), src[j][:, :, 0:HD],
                                             rden[:, j].unsqueeze(2).to_broadcast([T, HEADS, HD]), ALU.mult)
                last.then_inc(attn_ready, 1)

            def residual(im):
                s = im.slot(-1)
                n = im.index - 1
                if isinstance(n, int):
                    wait(dve, h1_saved[s], 16 * (n // 2))
                else:
                    dve.wait_ge(h1_saved[s], dve.snap((n - s) * 8))
                wait(dve, proj_ready, im.upto(-1))
                dve.scalar_tensor_tensor(h1[s].rearrange("p a b -> p (a b)"), W[0:T, 0:2 * D], 1.0 / (S_ACT * S_W),
                                         h0[im.slot(-1, 4)].rearrange("p a b -> p (a b)"),
                                         ALU.mult, ALU.add).then_inc(h1_ready, 1)

            def stats_h1(im):
                norm_stats(h1[im.slot(-1)], h1_ready, bn2, mv2, ln2_stat, im, -1)

            def norm_h1(im):
                wait(dve, y2T_ready, im.upto(-2))
                norm_apply(h1[im.slot(-1)], y2, mv2, rstd2, ln2_stat, y2_ready, im, -1)

            def low_y2(im, d):
                s = im.slot(d)
                wait(dve, y2T_high, im.upto(d))
                dve.scalar_tensor_tensor(y2T[s][:, :, 1], W[:, 0:2 * G].rearrange("p (k g) -> p k g", k=2), S_ACT,
                                         y2T[s][:, :, 0], ALU.mult, ALU.subtract).then_inc(y2T_split, 1)

            def gate_sums(im, d):
                n = im.index + d
                at = n if isinstance(n, int) else dve.snap(n)
                dst = gate_sum[:, at, :] if isinstance(n, int) else gate_sum[:, bass.ds(at, 1), :].rearrange("p o k -> p (o k)")
                wait(dve, y2T_high, im.upto(d))
                dve.tensor_copy(dst, token_sum).then_inc(gate_summed, 1)

            def expert_low(e):
                dve.wait_ge(high_taken, e + 1)
                dve.scalar_tensor_tensor(w1_all[:, e, 1, 0:FF], w1_raw[:, 0], S_W, w1_all[:, e, 0, 0:FF],
                                         ALU.mult, ALU.subtract)
                dve.scalar_tensor_tensor(w1_all[TAIL:128, e, 1, FF:2 * FF], w1_raw[TAIL:128, 1], S_W,
                                         w1_all[TAIL:128, e, 0, FF:2 * FF], ALU.mult, ALU.subtract)
                dve.scalar_tensor_tensor(w2_all[:, e, 1], w2_raw.rearrange("p c d -> p (c d)"), S_W,
                                         w2_all[:, e, 0], ALU.mult, ALU.subtract).then_inc(low_taken, 1)
                dve.wait_ge(low_taken, e + 1)
                rows, low_row, tail = slice(B1_HIGH, B1_LOW + 1), slice(B1_LOW, B1_LOW + 1), slice(FF, 2 * FF)
                dve.tensor_scalar(w1_all[rows, e, 0, tail], b1_raw[rows, e], S_W, None, ALU.mult).then_inc(b1_high, 1)
                dve.wait_ge(b1_high, e + 1)
                dve.scalar_tensor_tensor(w1_all[low_row, e, 0, tail], b1_raw[low_row, e], S_W,
                                         w1_all[low_row, e, 0, tail], ALU.mult, ALU.subtract).then_inc(b1_low, 1)

            zero = Image(dve, 0, 0)
            dve.wait_ge(patch_weights_ready, 1)
            low_x(zero, 0)
            self_step(dve.tensor_reduce(qkv_gs, qkv_raw[:, :, 0:2 * D].rearrange("p k (g e) -> p k g e", e=HD),
                                        AX_X, ALU.add))
            for k in range(NKC):
                self_step(dve.scalar_tensor_tensor(
                    qkv_raw[:, k, 0:2 * D].rearrange("p (g e) -> p g e", e=HD),
                    qkv_gs[:, k].unsqueeze(2).to_broadcast([KC, 2 * HEADS, HD]), -1.0 / HD,
                    qkv_raw[:, k, 0:2 * D].rearrange("p (g e) -> p g e", e=HD), ALU.mult, ALU.add))
            self_step(dve.tensor_scalar(qkv_w[:, 0], qkv_raw, S_W, None, ALU.mult))
            self_step(dve.scalar_tensor_tensor(qkv_w[:, 1], qkv_raw, S_W, qkv_w[:, 0], ALU.mult, ALU.subtract))
            self_step(dve.tensor_scalar(proj_w[:, 0], proj_raw, S_W, None, ALU.mult))
            dve.scalar_tensor_tensor(proj_w[:, 1], proj_raw, S_W, proj_w[:, 0], ALU.mult,
                                     ALU.subtract).then_inc(weights_ready, 1)
            token_stats(zero, 0)
            tokens(zero, 0)
            stats_tokens(zero, 0)
            norm_tokens(zero, 0)
            low(X, yT, yT_high, yT_split, zero, 0)
            sum_qk(zero, 0, 0)
            sum_qk(zero, 0, 1)
            norm_qk(zero, 0)
            low_x(zero, 1)
            low_qk(zero, 0, 0)
            low_qk(zero, 0, 1)
            token_stats(zero, 1)
            tokens(zero, 1)
            stats_tokens(zero, 1)
            dve.wait_ge(blanks_ready, BLANKS)
            queries(zero, 0, 0)
            queries(zero, 0, 1)
            norm_tokens(zero, 1)
            low(X, yT, yT_high, yT_split, zero, 1)
            low_x(zero, 2)

            def step(im, patches, prepare, project, finish):
                if prepare:
                    sum_qk(im, 1, 0)
                    sum_qk(im, 1, 1)
                    norm_qk(im, 1, im.has(3))
                if finish:
                    low_y2(im, -2)
                if patches:
                    token_stats(im, 2)
                if prepare:
                    low_qk(im, 1, 0)
                if finish:
                    gate_sums(im, -2)
                if prepare:
                    low_qk(im, 1, 1)
                if patches:
                    tokens(im, 2)
                if project:
                    low(W, aT, aT_high, aT_split, im, -1)
                if patches:
                    stats_tokens(im, 2)
                if prepare:
                    queries(im, 1, 0)
                if patches:
                    norm_tokens(im, 2)
                if project:
                    residual(im)
                    stats_h1(im)
                if patches:
                    low(X, yT, yT_high, yT_split, im, 2)
                if prepare:
                    queries(im, 1, 1)
                if project:
                    norm_h1(im)
                norm_attn(im, 0)
                if im.stands_at(B - 4):
                    expert_low(0)
                if im.stands_at(B - 3):
                    expert_low(1)
                if im.stands_at(B - 2):
                    expert_low(2)

            over_images(dve, step)
            last = Image(dve, B, 0)
            low_y2(last, -2)
            gate_sums(last, -2)
            low(W, aT, aT_high, aT_split, last, -1)
            residual(last)
            stats_h1(last)
            norm_h1(last)
            low_y2(last, -1)
            gate_sums(last, -1)

            dve.wait_ge(h1_saved[1], 16 * (B // 2))
            dve.wait_ge(o_ready[2], B)
            dve.wait_ge(aT_ready, B)
            dve.wait_ge(gate_summed, B)
            gates = [0]

            def gate_do(ins):
                gates[0] += 1
                ins.then_inc(gate_step, 1)
                dve.wait_ge(gate_step, gates[0])

            dve.wait_ge(logits_ready, 1)
            gate_do(dve.tensor_scalar(g_logit, X[0:B, 0:E], 1.0 / (G * S_ACT), None, ALU.mult))
            gate_do(dve.tensor_reduce(g_max, g_logit, AX_X, ALU.max))
            gate_do(dve.tensor_scalar(g_sub, g_logit, g_max[:, 0:1], None, ALU.subtract))
            gate_do(dve.tensor_scalar(g_is, g_sub, 0.0, None, ALU.is_ge))
            for n in range(2):
                gate_do(dve.tensor_scalar(g_not[:, n:n + 1], g_is[:, n:n + 1], -1.0, float(n + 1), ALU.mult, ALU.add))
            gate_do(dve.tensor_tensor(g_pair[:, 1:2], g_not[:, 0:1], g_not[:, 1:2], ALU.mult))
            dve.wait_ge(gate_exp, 1)
            gate_do(dve.tensor_reduce(g_sum, g_exp, AX_X, ALU.add))
            gate_do(dve.reciprocal(g_pair[:, 0:1], g_sum))
            dve.tensor_copy(g_wide, g_pair.unsqueeze(2).to_broadcast([B, 2, T])).then_inc(gate_wide, 1)
            dve.wait_ge(gate_ready, 1)
            gate_do(dve.tensor_copy(gate, Y[0:T, 0:B]))
            dve.tensor_copy(expert, Y[0:1, B:2 * B]).then_inc(expert_known, 1)
            dve.wait_ge(expert_known, 1)

            N1, N2 = 2 * NKC * FF, 2 * FC * D
            w1_flat = w1_all.rearrange("p e a n -> p (e a n)")
            w2_flat = w2_all.rearrange("p e a n -> p (e a n)")
            dve.wait_ge(low_taken, E)
            dve.wait_ge(b1_low, E)
            dve.wait_ge(stacked, E)

            def expert_of(im, d):
                n = im.index + d
                at = expert[0:1, n:n + 1] if isinstance(n, int) else expert[0:1, bass.ds(n, 1)]
                return dve.value_load(at, min_val=0, max_val=E - 1)

            def choose_w1(im, d, e):
                s = im.slot(d)
                wait(dve, hid_ready[2], im.upto(d - 2))
                dve.tensor_copy(w1_sel[s].rearrange("p a k f -> p (a k f)"),
                                w1_flat[:, bass.ds(dve.snap(e * N1), N1)]).then_inc(w1_chosen, 1)

            def choose_w2(im, d, e):
                s = im.slot(d)
                wait(dve, hid_used[2], im.upto(d - 2))
                dve.tensor_copy(w2_sel[s].rearrange("p a c d -> p (a c d)"),
                                w2_flat[:, bass.ds(dve.snap(e * N2), N2)]).then_inc(w2_chosen, 1)

            def low_hidden(im, d):
                for m in range(3):
                    wait(dve, hid_high[m], im.upto(d))
                    dve.scalar_tensor_tensor(hidT[m][:, 1], hid[m], S_HID, hidT[m][:, 0],
                                             ALU.mult, ALU.subtract).then_inc(hid_split[m], 1)

            def finish(im, e):
                s = im.slot(0)
                n = im.index
                bias = b2_all[:, bass.ds(dve.snap(e * D), D)]
                wait(dve, hid_used[2], im.upto(0))
                for j in range(2):
                    last = dve.scalar_tensor_tensor(y_out[s][:, j], bank[3 + 2 * s + j][0:T, 0:D], 1.0 / (S_HID * S_W),
                                                    bias, ALU.mult, ALU.add)
                last.then_inc(y_read, 1)
                if isinstance(n, int):
                    wait(dve, h1_back[s], 16 * (n // 2 + 1))
                    wait(dve, y_saved[s], 16 * (n // 2))
                else:
                    dve.wait_ge(h1_back[s], dve.snap((n - s) * 8 + 16))
                    dve.wait_ge(y_saved[s], dve.snap((n - s) * 8))
                wait(dve, y_read, im.upto(0))
                g = gate[:, n:n + 1] if isinstance(n, int) else gate[:, bass.ds(n, 1)]
                dve.scalar_tensor_tensor(y_fin[s], y_out[s], g, h1_in[s], ALU.mult, ALU.add).then_inc(y_done, 1)

            zero = Image(dve, 0, 0)
            for d in range(2):
                e = expert_of(zero, d)
                choose_w1(zero, d, e)
                choose_w2(zero, d, e)
            low_hidden(zero, 0)

            def step_2(im, more):
                if more:
                    ahead = expert_of(im, 2)
                    choose_w1(im, 2, ahead)
                if more or im.index + 1 < B:
                    low_hidden(im, 1)
                finish(im, expert_of(im, 0))
                if more:
                    choose_w2(im, 2, ahead)

            over_images_2(dve, step_2)

        @block.tensor
        def _(pe):
            def split_product(dst, left, right, cols, groups):
                pairs = [(a, b, k) for a, b in ((0, 0), (0, 1), (1, 0)) for k in range(groups)]
                for n, (a, b, k) in enumerate(pairs):
                    last = pe.matmul(dst, left(a, k), right(b, k)[:, cols], start=(n == 0), stop=(n == len(pairs) - 1))
                return last

            def model_product(dst, left, right, tail):
                steps = ((0, 0, 0, LEAD), (0, 1, 0, LEAD), (1, 0, 0, LEAD), (0, 1, 1, 2 * TAIL), (1, 0, 1, tail))
                for n, (x_half, w_half, chunk, rows) in enumerate(steps):
                    last = pe.matmul(dst, left(x_half, w_half, chunk, slice(0, rows)),
                                     right(x_half, w_half, chunk, slice(0, rows)), start=(n == 0), stop=(n == 4))
                return last

            pe.wait_ge(const_ready, CONSTS)
            pe.wait_ge(setup_dve, 2)
            for c in range(CB):
                pe.matmul(X[:, 0:D], ones[:, :], tok_full[:, c, 0:D], start=(c == 0), stop=(c == CB - 1))
            for c in range(CB):
                last = pe.matmul(Y[0:T, 0:D], beta_cols[:, c], tok_raw[:, c], start=(c == 0), stop=(c == CB - 1))
            last.then_inc(setup_mm, 1)

            def patches_mm(im, d, j):
                s = im.slot(d, 4)
                if j == 0:
                    wait(pe, x_split, im.upto(d))
                    wait(pe, v_ready, im.upto(d - 1))
                split_product(X[0:T, j * (D + 1):(j + 1) * (D + 1)],
                              lambda a, c: x_halves[s][:, a, c, j * T:(j + 1) * T],
                              lambda b, c: tok_w[:, b, c], slice(0, D + 1), CB)
                if j == 1:
                    wait(pe, xsq_summed, im.upto(d))
                    for jj in range(2):
                        last = pe.matmul(X[0:T, 2 * (D + 1) + jj:2 * (D + 1) + jj + 1],
                                         xsq_sum[:, jj * T:(jj + 1) * T], ones[:, 0:1], start=True, stop=True)
                    last.then_inc(tok_ready, 1)

            def turn(dst, src, done):
                for k in range(NKC):
                    for j in range(2):
                        last = pe.transpose(dst[0:KC, k * G + j * T:k * G + (j + 1) * T],
                                            src[:, j, k * KC:(k + 1) * KC], ident[0:T, 0:T])
                last.then_inc(done, 1)

            def turn_y(im, d):
                wait(pe, y_ready, im.upto(d))
                turn(X, y, yT_ready)

            def queries_keys_mm(im, d, j):
                if j == 0:
                    wait(pe, yT_split, im.upto(d))
                wait(pe, (k_ready, q_ready)[j][1], im.upto(d - 1))
                left = lambda a, k: yT[:, a, k * G + j * T:k * G + (j + 1) * T]
                right = lambda b, k: qkv_w[:, b, k]
                split_product((Y, Z)[j][0:T, 0:2 * D], left, right, slice(0, 2 * D), NKC).then_inc(qk_ready[j], 1)

            def values_mm(im, d):
                wait(pe, yT_split, im.upto(d))
                for j in range(2):
                    last = split_product(X[0:T, j * D:(j + 1) * D],
                                         lambda a, k: yT[:, a, k * G + j * T:k * G + (j + 1) * T],
                                         lambda b, k: qkv_w[:, b, k], slice(2 * D, 3 * D), NKC)
                last.then_inc(v_product, 1)

            def turn_qk(im, d, r):
                if r == 0:
                    for n in range(2):
                        wait(pe, qk_split[n], im.upto(d))
                else:
                    wait(pe, q_ready[0], im.upto(d))
                    wait(pe, k_ready[0], im.upto(d))
                for p in range(3):
                    for j in range(2):
                        h = j * HEADS + 2 * (3 * r + p)
                        at = slice(p * G + j * T, p * G + (j + 1) * T)
                        for dst, st in ((Z16, q_st), (Y16, k_st)):
                            last = pe.transpose(dst[:, at], st[:, h:h + 2, :].rearrange("p h e -> p (h e)"),
                                                ident16[0:T, 0:T])
                last.then_inc(stack_T[r], 1)

            def scores(im, d, h):
                s = im.slot(d)
                if h % 6 == 0:
                    wait(pe, q_ready[h // 6], im.upto(d))
                    wait(pe, k_ready[h // 6], im.upto(d))
                wait(pe, prob_ready[(h - 2) % HEADS], im.upto(d if h >= 2 else d - 1))
                rows = slice(64 * (h % 2), 64 * (h % 2) + 64)
                for k in range(2):
                    last = pe.matmul(S[h % 2][0:T, k * G:(k + 1) * G], kT[s][rows, h // 2, k * T:(k + 1) * T],
                                     qT[s][rows, h // 2, :], start=True, stop=True)
                last.then_inc(scores_ready[h], 1)

            def weigh(im, d, g):
                s = im.slot(d)
                wait(pe, prob_ready[4 * g + 3], im.upto(d))
                wait(pe, v_ready, im.upto(d))
                if g == 2:
                    wait(pe, o_out[0], im.upto(d))
                elif g == 0:
                    wait(pe, o_out[1], im.upto(d - 1))
                else:
                    wait(pe, o_out[2], im.upto(d - 1))
                    wait(pe, attn_ready, im.upto(d - 1))
                dst = o_bank(s, g)
                for k in range(2):
                    for q in range(4):
                        h = 4 * g + q
                        last = pe.matmul(dst[HW * q:HW * (q + 1), 0:G], val[s][:, k, h], prob[h][:, k * G:(k + 1) * G],
                                         start=(k == 0), stop=(k == 1))
                last.then_inc(o_ready[g], 1)

            def turn_o(im, d):
                wait(pe, o_out[2], im.upto(d))
                wait(pe, h1_ready, im.upto(d - 1))
                for j, dst in enumerate((W, o_bank(im.slot(d), 2))):
                    for g in range(3):
                        last = pe.transpose(dst[0:T, g * 128:(g + 1) * 128], oT[:, g, j * T:(j + 1) * T], ident[:, :])
                last.then_inc(o_tokens, 1)

            def turn_a(im):
                wait(pe, attn_ready, im.upto(-1))
                wait(pe, y2T_split, im.upto(-2))
                turn(W, attn, aT_ready)

            def project_mm(im):
                wait(pe, aT_split, im.upto(-1))
                for j in range(2):
                    last = split_product(W[0:T, j * D:(j + 1) * D],
                                         lambda a, k: aT[:, a, k * G + j * T:k * G + (j + 1) * T],
                                         lambda b, k: proj_w[:, b, k], slice(0, D), NKC)
                last.then_inc(proj_ready, 1)

            def turn_y2(im, d):
                wait(pe, y2_ready, im.upto(d))
                if im.has(d + 1):
                    wait(pe, attn_ready, im.upto(d + 1))
                for k, at in enumerate((0, D - LEAD)):
                    for j in range(2):
                        last = pe.transpose(W[:, k * G + j * T:k * G + (j + 1) * T], y2[:, j, at:at + LEAD],
                                            ident[0:T, 0:T])
                last.then_inc(y2T_ready, 1)

            pe.wait_ge(patch_weights_ready, 1)
            zero = Image(pe, 0, 0)
            patches_mm(zero, 0, 0)
            patches_mm(zero, 0, 1)
            turn_y(zero, 0)
            pe.wait_ge(weights_ready, 1)
            queries_keys_mm(zero, 0, 0)
            queries_keys_mm(zero, 0, 1)
            values_mm(zero, 0)
            patches_mm(zero, 1, 0)
            patches_mm(zero, 1, 1)
            turn_qk(zero, 0, 0)
            turn_qk(zero, 0, 1)
            scores(zero, 0, 0)
            scores(zero, 0, 1)
            turn_y(zero, 1)
            scores(zero, 0, 2)

            def step(im, patches, prepare, project, finish):
                scores(im, 0, 3)
                scores(im, 0, 4)
                if prepare:
                    queries_keys_mm(im, 1, 0)
                    queries_keys_mm(im, 1, 1)
                    values_mm(im, 1)
                if finish:
                    turn_y2(im, -2)
                scores(im, 0, 5)
                if patches:
                    patches_mm(im, 2, 0)
                scores(im, 0, 6)
                scores(im, 0, 7)
                if patches:
                    patches_mm(im, 2, 1)
                weigh(im, 0, 0)
                scores(im, 0, 8)
                scores(im, 0, 9)
                if project:
                    turn_a(im)
                weigh(im, 0, 1)
                if prepare:
                    turn_qk(im, 1, 0)
                scores(im, 0, 10)
                if project:
                    project_mm(im)
                scores(im, 0, 11)
                if prepare:
                    turn_qk(im, 1, 1)
                    scores(im, 1, 0)
                weigh(im, 0, 2)
                if prepare:
                    scores(im, 1, 1)
                if patches:
                    turn_y(im, 2)
                if prepare:
                    scores(im, 1, 2)
                turn_o(im, 0)

            over_images(pe, step)
            last = Image(pe, B, 0)
            turn_y2(last, -2)
            turn_a(last)
            project_mm(last)
            turn_y2(last, -1)

            pe.wait_ge(gate_summed, B)
            pe.wait_ge(h1_ready, B)
            for k in range(NKC):
                last = pe.matmul(X[0:B, 0:E], gate_sum[k * TAIL:128, :, k], gate_w[k * TAIL:128, k], start=(k == 0), stop=(k == NKC - 1))
            last.then_inc(logits_ready, 1)
            pe.wait_ge(gate_wide, 1)
            for n in range(2):
                last = pe.matmul(Y[0:T, n * B:(n + 1) * B], g_wide[:, n], ident[0:B, 0:B], start=True, stop=True)
            last.then_inc(gate_ready, 1)

            def first_product(im, d, m):
                s, s_x = im.slot(d), im.slot(d, 4)
                n = im.index + d
                if m == 0:
                    wait(pe, w1_chosen, im.upto(d))
                    if isinstance(n, int):
                        wait(pe, x2_in[s_x], 32 * (n // 4 + 1))
                    else:
                        pe.wait_ge(x2_in[s_x], pe.snap((n - s_x) * 8 + 32))
                wait(pe, hid_act[m], im.upto(d - 1))
                for c in range(2):
                    f = (2 * m + c) * 128
                    last = model_product(bank[m][:, c * G:(c + 1) * G],
                                         lambda a, b, k, rows: w1_sel[s][rows, b, k, f:f + 128],
                                         lambda a, b, k, rows: x2[s_x][rows, k, a], B1_LOW + 1)
                last.then_inc(hid_ready[m], 1)

            def second_product(im, m):
                s = im.slot(0)
                wait(pe, hid_split[m], im.upto(0))
                if m == 0:
                    wait(pe, w2_chosen, im.upto(0))
                    wait(pe, y_read, im.upto(-2))
                for c in range(2):
                    for j in range(2):
                        for n, (a, b) in enumerate(((0, 0), (0, 1), (1, 0))):
                            last = pe.matmul(bank[3 + 2 * s + j][0:T, 0:D],
                                             hidT[m][:, a, c * G + j * T:c * G + (j + 1) * T],
                                             w2_sel[s][:, b, 2 * m + c],
                                             start=(m == 0 and c == 0 and n == 0), stop=(m == 2 and c == 1 and n == 2))
                last.then_inc(hid_used[m], 1)

            zero = Image(pe, 0, 0)
            pe.wait_ge(rows_set, 12)
            pe.wait_ge(expert_known, 1)
            for m in range(3):
                first_product(zero, 0, m)

            def step_2(im, more):
                for m in range(3):
                    if more or im.index + 1 < B:
                        first_product(im, 1, m)
                    second_product(im, m)

            over_images_2(pe, step_2)


def kernel(x, L0_tok_gamma, L0_tok_beta, L0_tok_W, L0_tok_b, L0_attn_qkv_weight, L0_attn_proj_weight,
           L0_ffn_Wg, L0_ffn_W1, L0_ffn_b1, L0_ffn_W2, L0_ffn_b2):
    import numpy as np
    import concourse.bacc as bacc
    from concourse.bass_utils import run_bass_kernel_spmd

    x = np.asarray(x)
    B, C, H, W = x.shape
    R = H // PATCH
    parts = x.reshape(B, C, R, 2, HALF, R, 2, HALF).transpose(3, 6, 0, 4, 7, 1, 2, 5)
    own = np.ascontiguousarray(parts.transpose(2, 0, 3, 4, 5, 1, 6, 7)).reshape(B, 128, CH * 2, R * R)
    opposite = np.zeros((B, 2, HALF, HALF, C, 2, R + 1, R + 1), x.dtype)
    for a in range(2):
        for b in range(2):
            opposite[:, a, :, :, :, b, 1 - a:1 - a + R, 1 - b:1 - b + R] = parts[1 - a, 1 - b]
    opposite = opposite.reshape(B, 128, CH * 2 * (R + 1) * (R + 1))

    def by_pixel(v):
        v = np.asarray(v).reshape(-1, 2, HALF, 2, HALF, CH)
        return np.ascontiguousarray(v.transpose(1, 2, 4, 5, 3, 0)).reshape(128, CH * 2, -1)

    def tail_twice(v):
        lead, tail = v[..., 0:LEAD, :], v[..., LEAD:D, :]
        return np.ascontiguousarray(np.stack([lead, np.concatenate([tail, tail], axis=-2)], axis=-2))

    def by_chunk(v):
        v = np.asarray(v).T
        return np.ascontiguousarray(v.reshape(NKC, KC, -1).transpose(1, 0, 2))

    arrays = {
        "own": own, "opposite": opposite, "tok_W": by_pixel(L0_tok_W),
        "tok_gamma": by_pixel(L0_tok_gamma)[:, :, 0], "tok_beta": by_pixel(L0_tok_beta)[:, :, 0],
        "tok_b": np.asarray(L0_tok_b), "qkv_W": by_chunk(L0_attn_qkv_weight), "proj_W": by_chunk(L0_attn_proj_weight),
        "gate_W": tail_twice(np.asarray(L0_ffn_Wg).T), "W1": tail_twice(np.asarray(L0_ffn_W1)), "b1": np.asarray(L0_ffn_b1),
        "W2": np.asarray(L0_ffn_W2), "b2": np.asarray(L0_ffn_b2),
    }
    arrays = {k: np.ascontiguousarray(v) for k, v in arrays.items()}
    nc = bacc.Bacc("TRN2", target_bir_lowering=False, num_devices=1, dynamic_dma_scratch_size=1024)
    args = [nc.dram_tensor(f"in_{k}", v.shape, mybir.dt.from_np(v.dtype), kind="ExternalInput").ap()
            for k, v in arrays.items()]
    out = nc.dram_tensor("out_0", (B, R * R, D), F32, kind="ExternalOutput").ap()
    build_vit(nc, *args, out)
    r = run_bass_kernel_spmd(nc, [{f"in_{k}": v for k, v in arrays.items()}], core_ids=[0])
    return r.results[0]["out_0"]
```
